# Optimizing a Trainium2 kernel written in Bass

```python
import numpy as np
import jax
import jax.numpy as jnp

def _softmax(x, axis=-1):
    return jax.nn.softmax(x, axis=axis)

def _gelu(x):
    return jax.nn.gelu(x, approximate=True)

def _silu(x):
    return jax.nn.silu(x)

def _sigmoid(x):
    return jax.nn.sigmoid(x)

def _layernorm(x, axis=-1, eps=1e-05):
    m = jnp.mean(x, axis=axis, keepdims=True)
    v = jnp.var(x, axis=axis, keepdims=True)
    return (x - m) / jnp.sqrt(v + eps)

def _scatter_add(tgt, idx, src, axis=0):
    return tgt.at[idx].add(src)

def _segment_sum(src, seg, n):
    return jax.ops.segment_sum(src, seg, n)
kernel_name = 'mk_hybrid_d2_jaxref_r8_9925c2'

def setup_inputs(seed: int=0):
    np.random.seed(seed)
    _w = jnp.asarray

    def _L0_attn_a_setup():
        import math
        import jax, jax.numpy as jnp
        import numpy as np
        D_MODEL = 128
        N_HEADS = 16
        HEAD_DIM = D_MODEL // N_HEADS
        B, L = (1, 512)

        def _slopes(n_heads):
            ratio = 2.0 ** (-8.0 / n_heads)
            return jnp.asarray([ratio ** (i + 1) for i in range(n_heads)], dtype=jnp.float32)
        key = jax.random.key(seed)
        ks = jax.random.split(key, 5)
        scale = 1.0 / math.sqrt(D_MODEL)
        return {'x': jax.random.normal(ks[0], (B, L, D_MODEL), dtype=jnp.float32), 'q_w': jax.random.normal(ks[1], (D_MODEL, D_MODEL), dtype=jnp.float32) * scale, 'k_w': jax.random.normal(ks[2], (D_MODEL, D_MODEL), dtype=jnp.float32) * scale, 'v_w': jax.random.normal(ks[3], (D_MODEL, D_MODEL), dtype=jnp.float32) * scale, 'o_w': jax.random.normal(ks[4], (D_MODEL, D_MODEL), dtype=jnp.float32) * scale}
    _L0_attn_a_in = _L0_attn_a_setup()

    def _L0_attn_b_setup():
        import jax, jax.numpy as jnp
        import numpy as np
        H, DK, DV, CHUNK = (4, 32, 32, 32)

        def _silu(x):
            return x * jax.nn.sigmoid(x)

        def _l2norm(x, eps=1e-06):
            return x * jax.lax.rsqrt(jnp.sum(x * x, -1, keepdims=True) + eps)

        def _rmsnorm(x, w, eps=1e-05):
            return x * jax.lax.rsqrt(jnp.mean(x * x, -1, keepdims=True) + eps) * w

        def _causal_dwconv(x, w):
            C = x.shape[-1]
            K = w.shape[-1]
            xp = jnp.pad(x, ((0, 0), (K - 1, 0), (0, 0))).transpose(0, 2, 1)
            y = jax.lax.conv_general_dilated(xp, w[:, None, :], (1,), 'VALID', feature_group_count=C, dimension_numbers=('NCH', 'OIH', 'NCH'))
            return y.transpose(0, 2, 1)

        def _fir(x, filt):
            B, L, h, d = x.shape
            y = _causal_dwconv(x.reshape(B, L, h * d), filt.reshape(h * d, -1))
            return y.reshape(B, L, h, d)

        def _delta_rule_chunkwise(q, k, v, beta):
            b, h, L, dk = q.shape
            dv = v.shape[-1]
            n = L // CHUNK
            q = _l2norm(q)
            k = _l2norm(k)
            v = v * beta[..., None]
            k_beta = k * beta[..., None]
            rs = lambda t: t.reshape(b, h, n, CHUNK, -1)
            q, k, v, k_beta = (rs(q), rs(k), rs(v), rs(k_beta))
            eye = jnp.eye(CHUNK, dtype=q.dtype)
            strict_lower = jnp.tril(jnp.ones((CHUNK, CHUNK), bool), -1)
            A = jnp.where(strict_lower, jnp.einsum('bhncd,bhnsd->bhncs', k_beta, k), 0.0)
            attn_inv = jax.scipy.linalg.solve_triangular(eye + A, jnp.broadcast_to(eye, A.shape), lower=True)
            u = attn_inv @ v
            w = attn_inv @ k_beta
            incl_lower = jnp.tril(jnp.ones((CHUNK, CHUNK), bool))

            def step(S, inp):
                q_i, k_i, u_i, w_i = inp
                attn_local = jnp.where(incl_lower, q_i @ jnp.swapaxes(k_i, -1, -2), 0.0)
                u_t = u_i - w_i @ S
                o_i = q_i @ S + attn_local @ u_t
                return (S + jnp.swapaxes(k_i, -1, -2) @ u_t, o_i)
            S0 = jnp.zeros((b, h, dk, dv), q.dtype)
            xs = tuple((jnp.moveaxis(t, 2, 0) for t in (q, k, u, w)))
            S, out = jax.lax.scan(step, S0, xs)
            return (jnp.moveaxis(out, 0, 2).reshape(b, h, L, dv), S)

        def _stats(x):
            return jnp.stack([x.mean(-1), x.var(-1), jnp.abs(x).mean(-1), jnp.sqrt(jnp.sum(x * x, -1))], -1)

        def _forward(x, Wq, Wk, Wv, Wb, conv_q, conv_k, conv_v, fir_long, fir_short, W1, b1, W2, b2, log_temp, base_bias, conv_residual_logit, rms_w, Wo):
            B, L, D = x.shape
            q = _silu(_causal_dwconv(x @ Wq, conv_q)).reshape(B, L, H, DK)
            k = _silu(_causal_dwconv(x @ Wk, conv_k)).reshape(B, L, H, DK)
            v = _silu(_causal_dwconv(x @ Wv, conv_v)).reshape(B, L, H, DV)
            beta = jax.nn.sigmoid(x @ Wb)
            delta, _S = _delta_rule_chunkwise(q.transpose(0, 2, 1, 3), k.transpose(0, 2, 1, 3), v.transpose(0, 2, 1, 3), beta.transpose(0, 2, 1))
            delta = delta.transpose(0, 2, 1, 3)
            f_short = _fir(v, fir_short)
            f_long = _fir(v, fir_long)
            stats = jnp.concatenate([_stats(f_short), _stats(f_long), _stats(delta), _stats(v)], -1)
            hidden_exp = jnp.broadcast_to(x[:, :, None, :], (B, L, H, D))
            gate_in = jnp.concatenate([hidden_exp, stats], -1)
            h1 = jax.nn.gelu(gate_in @ W1 + b1, approximate=False)
            logits = h1 @ W2 + b2 + base_bias
            temp = jax.nn.softplus(log_temp) + 0.0001
            p = jax.nn.softmax(logits / temp[:, None], -1)
            eps = 0.05
            p = jnp.maximum(p, jnp.array([eps, eps, 0.0, 0.0], p.dtype))
            p = p / jnp.sum(p, -1, keepdims=True)
            o = p[..., 0:1] * f_short + p[..., 1:2] * f_long + p[..., 2:3] * delta + p[..., 3:4] * v
            o = o + 0.5 * jax.nn.sigmoid(conv_residual_logit)[None, None, :, None] * f_short
            o = _rmsnorm(o, rms_w)
            return o.reshape(B, L, H * DV) @ Wo
        key = jax.random.key(seed)
        ks = jax.random.split(key, 13)
        B, L, D = (2, 256, 128)
        f = jnp.float32
        n = lambda k, shape, s=0.02: jax.random.normal(k, shape, f) * s
        return {'x': jax.random.normal(ks[0], (B, L, D), f), 'Wq': n(ks[1], (D, D)), 'Wk': n(ks[2], (D, D)), 'Wv': n(ks[3], (D, D)), 'Wb': n(ks[4], (D, H)), 'conv_q': n(ks[5], (D, 4), 0.1), 'conv_k': n(ks[6], (D, 4), 0.1), 'conv_v': n(ks[7], (D, 4), 0.1), 'fir_long': n(ks[8], (H, DV, 64)), 'fir_short': n(ks[9], (H, DV, 5)), 'W1': n(ks[10], (D + 16, D)), 'b1': jnp.zeros((D,), f), 'W2': n(ks[11], (D, 4)), 'b2': jnp.zeros((4,), f), 'log_temp': jnp.full((H,), float(np.log(np.expm1(0.7))), f), 'base_bias': jnp.tile(jnp.array([-0.5, -0.5, 1.0, 3.0], f), (H, 1)), 'conv_residual_logit': jnp.full((H,), -2.0, f), 'rms_w': jnp.ones((DV,), f), 'Wo': n(ks[12], (D, D))}
    _L0_attn_b_in = _L0_attn_b_setup()

    def _L0_ffn_setup():
        import jax, jax.numpy as jnp
        import numpy as np
        DIM = 128
        HIDDEN = 384
        SCALE = 1.0 / 127.0

        def _dequant(w_int, dtype):
            return w_int.astype(dtype) * jnp.asarray(SCALE, dtype)
        key = jax.random.key(seed)
        k_x, k_g, k_u, k_d = jax.random.split(key, 4)
        x = jax.random.normal(k_x, (4, 256, DIM), dtype=jnp.float32)
        w_gate = jax.random.randint(k_g, (HIDDEN, DIM), -127, 128, dtype=jnp.int32)
        w_up = jax.random.randint(k_u, (HIDDEN, DIM), -127, 128, dtype=jnp.int32)
        w_down = jax.random.randint(k_d, (DIM, HIDDEN), -127, 128, dtype=jnp.int32)
        return {'x': x, 'w_gate': w_gate, 'w_up': w_up, 'w_down': w_down}
    _L0_ffn_in = _L0_ffn_setup()

    def _L1_attn_a_setup():
        import jax, jax.numpy as jnp
        import numpy as np
        D_MODEL = 128
        D_STATE = 64
        D_CONV = 7
        EXPAND = 2
        HEADDIM = 64
        NGROUPS = 1
        D_INNER = EXPAND * D_MODEL
        NHEADS = D_INNER // HEADDIM
        D_IN_PROJ = 2 * D_INNER + 2 * (2 * NGROUPS * D_STATE) + 2 * NHEADS
        CONV_DIM = D_INNER + 2 * (2 * NGROUPS * D_STATE)
        BATCH = 2
        SEQLEN = 256
        EPS = 1e-05
        key = jax.random.key(seed)
        ks = jax.random.split(key, 8)
        u = jax.random.normal(ks[0], (BATCH, SEQLEN, D_MODEL), jnp.float32)
        W_in = jax.random.normal(ks[1], (D_IN_PROJ, D_MODEL), jnp.float32) * 0.02
        conv_w = jax.random.normal(ks[2], (CONV_DIM, 1, D_CONV), jnp.float32) * 0.2
        conv_b = jax.random.normal(ks[3], (CONV_DIM,), jnp.float32) * 0.02
        dt = jnp.exp(jax.random.uniform(ks[4], (NHEADS,)) * (np.log(0.1) - np.log(0.001)) + np.log(0.001))
        dt = jnp.clip(dt, 0.0001)
        dt_bias = dt + jnp.log(-jnp.expm1(-dt))
        A_log = jnp.zeros((NHEADS,), jnp.float32)
        Dp = jnp.ones((NHEADS,), jnp.float32)
        fc_D_w = jax.random.normal(ks[5], (NHEADS, D_INNER), jnp.float32) * 0.02
        norm_w = jnp.ones((D_INNER,), jnp.float32)
        W_out = jax.random.normal(ks[6], (D_MODEL, D_INNER), jnp.float32) * 0.02
        return dict(u=u, W_in=W_in, conv_w=conv_w, conv_b=conv_b, dt_bias=dt_bias, A_log=A_log, Dp=Dp, fc_D_w=fc_D_w, norm_w=norm_w, W_out=W_out)
    _L1_attn_a_in = _L1_attn_a_setup()

    def _L1_attn_b_setup():
        import jax, jax.numpy as jnp
        import numpy as np
        NUM_HEADS = 16
        EPS = float(jnp.finfo(jnp.float32).eps)

        def rms_norm(x, w):
            ms = jnp.mean(x * x, axis=-1, keepdims=True)
            return x * jax.lax.rsqrt(ms + EPS) * w
        key = jax.random.key(seed)
        k = jax.random.split(key, 5)
        B, N, D = (4, 256, 128)
        Dh = D // NUM_HEADS
        return {'x': jax.random.normal(k[0], (B, N, D), dtype=jnp.float32), 'Wq': jax.random.normal(k[1], (D, D), dtype=jnp.float32) * 0.02, 'Wk': jax.random.normal(k[2], (D, D), dtype=jnp.float32) * 0.02, 'Wv': jax.random.normal(k[3], (D, D), dtype=jnp.float32) * 0.02, 'Wo': jax.random.normal(k[4], (D, D), dtype=jnp.float32) * 0.02, 'qn_w': jnp.ones((Dh,), dtype=jnp.float32), 'kn_w': jnp.ones((Dh,), dtype=jnp.float32)}
    _L1_attn_b_in = _L1_attn_b_setup()

    def _L1_ffn_setup():
        import jax, jax.numpy as jnp
        import numpy as np
        D_MODEL = 128
        N_HEAD = 16
        HEAD_DIM = D_MODEL // N_HEAD
        D_FF = 512
        N_EXPERTS = 4
        EPS = 1e-05

        def _layer_norm(x, gamma, beta):
            mu = jnp.mean(x, axis=-1, keepdims=True)
            var = jnp.mean((x - mu) ** 2, axis=-1, keepdims=True)
            return (x - mu) / jnp.sqrt(var + EPS) * gamma + beta
        key = jax.random.key(seed)
        ks = jax.random.split(key, 20)
        f32 = jnp.float32
        sc = 1.0 / np.sqrt(D_MODEL)
        scf = 1.0 / np.sqrt(D_FF)
        return {'src': jax.random.normal(ks[0], (4, 64, D_MODEL), f32), 'Wq': jax.random.normal(ks[1], (D_MODEL, D_MODEL), f32) * sc, 'bq': jnp.zeros((D_MODEL,), f32), 'Wk': jax.random.normal(ks[2], (D_MODEL, D_MODEL), f32) * sc, 'bk': jnp.zeros((D_MODEL,), f32), 'Wv': jax.random.normal(ks[3], (D_MODEL, D_MODEL), f32) * sc, 'bv': jnp.zeros((D_MODEL,), f32), 'Wo': jax.random.normal(ks[4], (D_MODEL, D_MODEL), f32) * sc, 'bo': jnp.zeros((D_MODEL,), f32), 'router_w': jax.random.normal(ks[5], (D_MODEL, 1), f32) * 0.05, 'router_b': jnp.zeros((1,), f32), 'W1': jax.random.normal(ks[6], (N_EXPERTS, D_MODEL, D_FF), f32) * sc, 'b1': jnp.zeros((N_EXPERTS, D_FF), f32), 'W2': jax.random.normal(ks[7], (N_EXPERTS, D_FF, D_MODEL), f32) * scf, 'b2': jnp.zeros((N_EXPERTS, D_MODEL), f32), 'ln1_g': jnp.ones((D_MODEL,), f32), 'ln1_b': jnp.zeros((D_MODEL,), f32), 'ln2_g': jnp.ones((D_MODEL,), f32), 'ln2_b': jnp.zeros((D_MODEL,), f32)}
    _L1_ffn_in = _L1_ffn_setup()
    _d = {'L0_attn_a_x': _L0_attn_a_in['x'], 'L0_attn_a_q_w': _L0_attn_a_in['q_w'], 'L0_attn_a_k_w': _L0_attn_a_in['k_w'], 'L0_attn_a_v_w': _L0_attn_a_in['v_w'], 'L0_attn_a_o_w': _L0_attn_a_in['o_w'], 'L0_attn_b_Wq': _L0_attn_b_in['Wq'], 'L0_attn_b_Wk': _L0_attn_b_in['Wk'], 'L0_attn_b_Wv': _L0_attn_b_in['Wv'], 'L0_attn_b_Wb': _L0_attn_b_in['Wb'], 'L0_attn_b_conv_q': _L0_attn_b_in['conv_q'], 'L0_attn_b_conv_k': _L0_attn_b_in['conv_k'], 'L0_attn_b_conv_v': _L0_attn_b_in['conv_v'], 'L0_attn_b_fir_long': _L0_attn_b_in['fir_long'], 'L0_attn_b_fir_short': _L0_attn_b_in['fir_short'], 'L0_attn_b_W1': _L0_attn_b_in['W1'], 'L0_attn_b_b1': _L0_attn_b_in['b1'], 'L0_attn_b_W2': _L0_attn_b_in['W2'], 'L0_attn_b_b2': _L0_attn_b_in['b2'], 'L0_attn_b_log_temp': _L0_attn_b_in['log_temp'], 'L0_attn_b_base_bias': _L0_attn_b_in['base_bias'], 'L0_attn_b_conv_residual_logit': _L0_attn_b_in['conv_residual_logit'], 'L0_attn_b_rms_w': _L0_attn_b_in['rms_w'], 'L0_attn_b_Wo': _L0_attn_b_in['Wo'], 'L0_ffn_w_gate': _L0_ffn_in['w_gate'], 'L0_ffn_w_up': _L0_ffn_in['w_up'], 'L0_ffn_w_down': _L0_ffn_in['w_down'], 'L1_attn_a_W_in': _L1_attn_a_in['W_in'], 'L1_attn_a_conv_w': _L1_attn_a_in['conv_w'], 'L1_attn_a_conv_b': _L1_attn_a_in['conv_b'], 'L1_attn_a_dt_bias': _L1_attn_a_in['dt_bias'], 'L1_attn_a_A_log': _L1_attn_a_in['A_log'], 'L1_attn_a_Dp': _L1_attn_a_in['Dp'], 'L1_attn_a_fc_D_w': _L1_attn_a_in['fc_D_w'], 'L1_attn_a_norm_w': _L1_attn_a_in['norm_w'], 'L1_attn_a_W_out': _L1_attn_a_in['W_out'], 'L1_attn_b_Wq': _L1_attn_b_in['Wq'], 'L1_attn_b_Wk': _L1_attn_b_in['Wk'], 'L1_attn_b_Wv': _L1_attn_b_in['Wv'], 'L1_attn_b_Wo': _L1_attn_b_in['Wo'], 'L1_attn_b_qn_w': _L1_attn_b_in['qn_w'], 'L1_attn_b_kn_w': _L1_attn_b_in['kn_w'], 'L1_ffn_Wq': _L1_ffn_in['Wq'], 'L1_ffn_bq': _L1_ffn_in['bq'], 'L1_ffn_Wk': _L1_ffn_in['Wk'], 'L1_ffn_bk': _L1_ffn_in['bk'], 'L1_ffn_Wv': _L1_ffn_in['Wv'], 'L1_ffn_bv': _L1_ffn_in['bv'], 'L1_ffn_Wo': _L1_ffn_in['Wo'], 'L1_ffn_bo': _L1_ffn_in['bo'], 'L1_ffn_router_w': _L1_ffn_in['router_w'], 'L1_ffn_router_b': _L1_ffn_in['router_b'], 'L1_ffn_W1': _L1_ffn_in['W1'], 'L1_ffn_b1': _L1_ffn_in['b1'], 'L1_ffn_W2': _L1_ffn_in['W2'], 'L1_ffn_b2': _L1_ffn_in['b2'], 'L1_ffn_ln1_g': _L1_ffn_in['ln1_g'], 'L1_ffn_ln1_b': _L1_ffn_in['ln1_b'], 'L1_ffn_ln2_g': _L1_ffn_in['ln2_g'], 'L1_ffn_ln2_b': _L1_ffn_in['ln2_b']}
    _x0 = _d['L0_attn_a_x']
    _d['L0_attn_a_x'] = jax.random.normal(jax.random.fold_in(jax.random.key(seed), 1), (4, 1024, 128), dtype=_x0.dtype)
    del _x0
    return _d

def reference(L0_attn_a_x, L0_attn_a_q_w, L0_attn_a_k_w, L0_attn_a_v_w, L0_attn_a_o_w, L0_attn_b_Wq, L0_attn_b_Wk, L0_attn_b_Wv, L0_attn_b_Wb, L0_attn_b_conv_q, L0_attn_b_conv_k, L0_attn_b_conv_v, L0_attn_b_fir_long, L0_attn_b_fir_short, L0_attn_b_W1, L0_attn_b_b1, L0_attn_b_W2, L0_attn_b_b2, L0_attn_b_log_temp, L0_attn_b_base_bias, L0_attn_b_conv_residual_logit, L0_attn_b_rms_w, L0_attn_b_Wo, L0_ffn_w_gate, L0_ffn_w_up, L0_ffn_w_down, L1_attn_a_W_in, L1_attn_a_conv_w, L1_attn_a_conv_b, L1_attn_a_dt_bias, L1_attn_a_A_log, L1_attn_a_Dp, L1_attn_a_fc_D_w, L1_attn_a_norm_w, L1_attn_a_W_out, L1_attn_b_Wq, L1_attn_b_Wk, L1_attn_b_Wv, L1_attn_b_Wo, L1_attn_b_qn_w, L1_attn_b_kn_w, L1_ffn_Wq, L1_ffn_bq, L1_ffn_Wk, L1_ffn_bk, L1_ffn_Wv, L1_ffn_bv, L1_ffn_Wo, L1_ffn_bo, L1_ffn_router_w, L1_ffn_router_b, L1_ffn_W1, L1_ffn_b1, L1_ffn_W2, L1_ffn_b2, L1_ffn_ln1_g, L1_ffn_ln1_b, L1_ffn_ln2_g, L1_ffn_ln2_b):

    def _L0_attn_a_ref(x, q_w, k_w, v_w, o_w):
        import math
        import jax, jax.numpy as jnp
        import numpy as np
        D_MODEL = 128
        N_HEADS = 16
        HEAD_DIM = D_MODEL // N_HEADS
        B, L = (1, 512)

        def _slopes(n_heads):
            ratio = 2.0 ** (-8.0 / n_heads)
            return jnp.asarray([ratio ** (i + 1) for i in range(n_heads)], dtype=jnp.float32)
        b, l, _ = x.shape

        def proj(w):
            return (x @ w).reshape(b, l, N_HEADS, HEAD_DIM).transpose(0, 2, 1, 3)
        q, k, v = (proj(q_w), proj(k_w), proj(v_w))
        scale = math.sqrt(HEAD_DIM)
        scores = jnp.einsum('bhid,bhjd->bhij', q, k) / scale
        pos = jnp.arange(l)
        distance = jnp.abs(pos[None, :] - pos[:, None]).astype(jnp.float32)
        alibi = -distance[None, :, :] * _slopes(N_HEADS)[:, None, None]
        scores = scores + alibi[None]
        causal = pos[None, :] <= pos[:, None]
        scores = jnp.where(causal[None, None], scores, -jnp.inf)
        attn = jax.nn.softmax(scores, axis=-1)
        out = jnp.einsum('bhij,bhjd->bhid', attn, v)
        out = out.transpose(0, 2, 1, 3).reshape(b, l, D_MODEL)
        return out @ o_w

    def _L0_attn_b_ref(x, Wq, Wk, Wv, Wb, conv_q, conv_k, conv_v, fir_long, fir_short, W1, b1, W2, b2, log_temp, base_bias, conv_residual_logit, rms_w, Wo):
        import jax, jax.numpy as jnp
        import numpy as np
        H, DK, DV, CHUNK = (4, 32, 32, 32)

        def _silu(x):
            return x * jax.nn.sigmoid(x)

        def _l2norm(x, eps=1e-06):
            return x * jax.lax.rsqrt(jnp.sum(x * x, -1, keepdims=True) + eps)

        def _rmsnorm(x, w, eps=1e-05):
            return x * jax.lax.rsqrt(jnp.mean(x * x, -1, keepdims=True) + eps) * w

        def _causal_dwconv(x, w):
            C = x.shape[-1]
            K = w.shape[-1]
            xp = jnp.pad(x, ((0, 0), (K - 1, 0), (0, 0))).transpose(0, 2, 1)
            y = jax.lax.conv_general_dilated(xp, w[:, None, :], (1,), 'VALID', feature_group_count=C, dimension_numbers=('NCH', 'OIH', 'NCH'))
            return y.transpose(0, 2, 1)

        def _fir(x, filt):
            B, L, h, d = x.shape
            y = _causal_dwconv(x.reshape(B, L, h * d), filt.reshape(h * d, -1))
            return y.reshape(B, L, h, d)

        def _delta_rule_chunkwise(q, k, v, beta):
            b, h, L, dk = q.shape
            dv = v.shape[-1]
            n = L // CHUNK
            q = _l2norm(q)
            k = _l2norm(k)
            v = v * beta[..., None]
            k_beta = k * beta[..., None]
            rs = lambda t: t.reshape(b, h, n, CHUNK, -1)
            q, k, v, k_beta = (rs(q), rs(k), rs(v), rs(k_beta))
            eye = jnp.eye(CHUNK, dtype=q.dtype)
            strict_lower = jnp.tril(jnp.ones((CHUNK, CHUNK), bool), -1)
            A = jnp.where(strict_lower, jnp.einsum('bhncd,bhnsd->bhncs', k_beta, k), 0.0)
            attn_inv = jax.scipy.linalg.solve_triangular(eye + A, jnp.broadcast_to(eye, A.shape), lower=True)
            u = attn_inv @ v
            w = attn_inv @ k_beta
            incl_lower = jnp.tril(jnp.ones((CHUNK, CHUNK), bool))

            def step(S, inp):
                q_i, k_i, u_i, w_i = inp
                attn_local = jnp.where(incl_lower, q_i @ jnp.swapaxes(k_i, -1, -2), 0.0)
                u_t = u_i - w_i @ S
                o_i = q_i @ S + attn_local @ u_t
                return (S + jnp.swapaxes(k_i, -1, -2) @ u_t, o_i)
            S0 = jnp.zeros((b, h, dk, dv), q.dtype)
            xs = tuple((jnp.moveaxis(t, 2, 0) for t in (q, k, u, w)))
            S, out = jax.lax.scan(step, S0, xs)
            return (jnp.moveaxis(out, 0, 2).reshape(b, h, L, dv), S)

        def _stats(x):
            return jnp.stack([x.mean(-1), x.var(-1), jnp.abs(x).mean(-1), jnp.sqrt(jnp.sum(x * x, -1))], -1)

        def _forward(x, Wq, Wk, Wv, Wb, conv_q, conv_k, conv_v, fir_long, fir_short, W1, b1, W2, b2, log_temp, base_bias, conv_residual_logit, rms_w, Wo):
            B, L, D = x.shape
            q = _silu(_causal_dwconv(x @ Wq, conv_q)).reshape(B, L, H, DK)
            k = _silu(_causal_dwconv(x @ Wk, conv_k)).reshape(B, L, H, DK)
            v = _silu(_causal_dwconv(x @ Wv, conv_v)).reshape(B, L, H, DV)
            beta = jax.nn.sigmoid(x @ Wb)
            delta, _S = _delta_rule_chunkwise(q.transpose(0, 2, 1, 3), k.transpose(0, 2, 1, 3), v.transpose(0, 2, 1, 3), beta.transpose(0, 2, 1))
            delta = delta.transpose(0, 2, 1, 3)
            f_short = _fir(v, fir_short)
            f_long = _fir(v, fir_long)
            stats = jnp.concatenate([_stats(f_short), _stats(f_long), _stats(delta), _stats(v)], -1)
            hidden_exp = jnp.broadcast_to(x[:, :, None, :], (B, L, H, D))
            gate_in = jnp.concatenate([hidden_exp, stats], -1)
            h1 = jax.nn.gelu(gate_in @ W1 + b1, approximate=False)
            logits = h1 @ W2 + b2 + base_bias
            temp = jax.nn.softplus(log_temp) + 0.0001
            p = jax.nn.softmax(logits / temp[:, None], -1)
            eps = 0.05
            p = jnp.maximum(p, jnp.array([eps, eps, 0.0, 0.0], p.dtype))
            p = p / jnp.sum(p, -1, keepdims=True)
            o = p[..., 0:1] * f_short + p[..., 1:2] * f_long + p[..., 2:3] * delta + p[..., 3:4] * v
            o = o + 0.5 * jax.nn.sigmoid(conv_residual_logit)[None, None, :, None] * f_short
            o = _rmsnorm(o, rms_w)
            return o.reshape(B, L, H * DV) @ Wo
        return _forward(x, Wq, Wk, Wv, Wb, conv_q, conv_k, conv_v, fir_long, fir_short, W1, b1, W2, b2, log_temp, base_bias, conv_residual_logit, rms_w, Wo)

    def _L0_ffn_ref(x, w_gate, w_up, w_down):
        import jax, jax.numpy as jnp
        import numpy as np
        DIM = 128
        HIDDEN = 384
        SCALE = 1.0 / 127.0

        def _dequant(w_int, dtype):
            return w_int.astype(dtype) * jnp.asarray(SCALE, dtype)
        wg = _dequant(w_gate, x.dtype)
        wu = _dequant(w_up, x.dtype)
        wd = _dequant(w_down, x.dtype)
        gate = jnp.einsum('bsd,hd->bsh', x, wg)
        up = jnp.einsum('bsd,hd->bsh', x, wu)
        h = jax.nn.silu(gate) * up
        return jnp.einsum('bsh,dh->bsd', h, wd)

    def _L1_attn_a_ref(u, W_in, conv_w, conv_b, dt_bias, A_log, Dp, fc_D_w, norm_w, W_out):
        import jax, jax.numpy as jnp
        import numpy as np
        D_MODEL = 128
        D_STATE = 64
        D_CONV = 7
        EXPAND = 2
        HEADDIM = 64
        NGROUPS = 1
        D_INNER = EXPAND * D_MODEL
        NHEADS = D_INNER // HEADDIM
        D_IN_PROJ = 2 * D_INNER + 2 * (2 * NGROUPS * D_STATE) + 2 * NHEADS
        CONV_DIM = D_INNER + 2 * (2 * NGROUPS * D_STATE)
        BATCH = 2
        SEQLEN = 256
        EPS = 1e-05
        b, L, _ = u.shape
        gn = NGROUPS * D_STATE
        zxbcdt = jnp.einsum('bld,ed->ble', u, W_in)
        A = -jnp.exp(A_log)
        z = zxbcdt[..., :D_INNER]
        xBC = zxbcdt[..., D_INNER:D_INNER + CONV_DIM]
        dt_raw = zxbcdt[..., D_INNER + CONV_DIM:]
        dt = jnp.concatenate([dt_raw[..., :NHEADS], dt_raw[..., NHEADS:][:, ::-1]], axis=0)
        dt = jax.nn.softplus(dt + dt_bias)
        xc = jnp.transpose(xBC, (0, 2, 1))
        xc = jax.lax.conv_general_dilated(xc, conv_w, (1,), [(D_CONV // 2, D_CONV // 2)], dimension_numbers=('NCH', 'OIH', 'NCH'), feature_group_count=CONV_DIM)
        xc = xc + conv_b[None, :, None]
        xBC = jax.nn.silu(jnp.transpose(xc, (0, 2, 1)))
        x = xBC[..., :D_INNER]
        BC = xBC[..., D_INNER:]
        x_og = x
        x2 = jnp.concatenate([x, x[:, ::-1]], axis=0)
        BC2 = jnp.concatenate([BC[..., :2 * gn], BC[..., 2 * gn:][:, ::-1]], axis=0)
        Bm = BC2[..., :gn].reshape(2 * b, L, NGROUPS, D_STATE)
        Cm = BC2[..., gn:].reshape(2 * b, L, NGROUPS, D_STATE)
        x_scan = x2.reshape(2 * b, L, NHEADS, HEADDIM)
        hpg = NHEADS // NGROUPS
        Bh = jnp.repeat(Bm, hpg, axis=2)
        Ch = jnp.repeat(Cm, hpg, axis=2)

        def step(state, ins):
            x_t, dt_t, B_t, C_t = ins
            ex = jnp.exp(A[None, :, None, None] * dt_t[:, :, None, None])
            state = state * ex + x_t[..., None] * B_t[:, :, None, :]
            y_t = jnp.sum(state * C_t[:, :, None, :], axis=-1)
            return (state, y_t)
        xs = (jnp.moveaxis(x_scan, 1, 0), jnp.moveaxis(dt, 1, 0), jnp.moveaxis(Bh, 1, 0), jnp.moveaxis(Ch, 1, 0))
        state0 = jnp.zeros((2 * b, NHEADS, HEADDIM, D_STATE), u.dtype)
        _, ys = jax.lax.scan(step, state0, xs)
        y = jnp.moveaxis(ys, 0, 1).reshape(2 * b, L, D_INNER)
        y = jnp.concatenate([jnp.zeros_like(y[:, :1]), y[:, :-1]], axis=1)
        y_fw, y_bw = (y[:b], y[b:][:, ::-1])
        diag_heads = jnp.einsum('bld,hd->blh', x_og, fc_D_w) + Dp
        diag = jnp.repeat(diag_heads, HEADDIM, axis=-1)
        y = y_fw + y_bw + x_og * diag
        rms = jnp.sqrt(jnp.mean(y * y, axis=-1, keepdims=True) + EPS)
        y = norm_w * (y / rms) * jax.nn.silu(z)
        return jnp.einsum('ble,de->bld', y, W_out)

    def _L1_attn_b_ref(x, Wq, Wk, Wv, Wo, qn_w, kn_w):
        import jax, jax.numpy as jnp
        import numpy as np
        NUM_HEADS = 16
        EPS = float(jnp.finfo(jnp.float32).eps)

        def rms_norm(x, w):
            ms = jnp.mean(x * x, axis=-1, keepdims=True)
            return x * jax.lax.rsqrt(ms + EPS) * w
        B, N, D = x.shape
        H = NUM_HEADS
        Dh = D // H
        scale = Dh ** (-0.5)

        def proj(W):
            return (x @ W.T).reshape(B, N, H, Dh).transpose(0, 2, 1, 3)
        q = rms_norm(proj(Wq), qn_w)
        k = rms_norm(proj(Wk), kn_w)
        v = proj(Wv)
        scores = jnp.einsum('bhnd,bhmd->bhnm', q, k) * scale
        attn = jax.nn.softmax(scores, axis=-1)
        out = jnp.einsum('bhnm,bhmd->bhnd', attn, v)
        out = out.transpose(0, 2, 1, 3).reshape(B, N, D)
        return out @ Wo.T

    def _L1_ffn_ref(src, Wq, bq, Wk, bk, Wv, bv, Wo, bo, router_w, router_b, W1, b1, W2, b2, ln1_g, ln1_b, ln2_g, ln2_b):
        import jax, jax.numpy as jnp
        import numpy as np
        D_MODEL = 128
        N_HEAD = 16
        HEAD_DIM = D_MODEL // N_HEAD
        D_FF = 512
        N_EXPERTS = 4
        EPS = 1e-05

        def _layer_norm(x, gamma, beta):
            mu = jnp.mean(x, axis=-1, keepdims=True)
            var = jnp.mean((x - mu) ** 2, axis=-1, keepdims=True)
            return (x - mu) / jnp.sqrt(var + EPS) * gamma + beta
        B, T, _ = src.shape
        q = (src @ Wq + bq).reshape(B, T, N_HEAD, HEAD_DIM)
        k = (src @ Wk + bk).reshape(B, T, N_HEAD, HEAD_DIM)
        v = (src @ Wv + bv).reshape(B, T, N_HEAD, HEAD_DIM)
        scale = HEAD_DIM ** (-0.5)
        scores = jnp.einsum('bqhd,bkhd->bhqk', q, k) * scale
        probs = jax.nn.softmax(scores, axis=-1)
        attn = jnp.einsum('bhqk,bkhd->bqhd', probs, v).reshape(B, T, D_MODEL)
        attn = attn @ Wo + bo
        x = _layer_norm(src + attn, ln1_g, ln1_b)
        keys = (x @ router_w + router_b)[..., 0]
        expert_idx = jnp.remainder(jnp.floor(keys).astype(jnp.int32), N_EXPERTS)
        ff_out = jnp.zeros_like(x)
        for e in range(N_EXPERTS):
            h = jax.nn.relu(x @ W1[e] + b1[e])
            y = h @ W2[e] + b2[e]
            ff_out = ff_out + jnp.where((expert_idx == e)[..., None], y, 0.0)
        return _layer_norm(x + ff_out, ln2_g, ln2_b)
    x = L0_attn_a_x
    x = x + _L0_attn_a_ref(_layernorm(x, axis=-1), L0_attn_a_q_w, L0_attn_a_k_w, L0_attn_a_v_w, L0_attn_a_o_w)
    x = x + _L0_ffn_ref(_layernorm(x, axis=-1), L0_ffn_w_gate, L0_ffn_w_up, L0_ffn_w_down)
    x = x + _L0_attn_b_ref(_layernorm(x, axis=-1), L0_attn_b_Wq, L0_attn_b_Wk, L0_attn_b_Wv, L0_attn_b_Wb, L0_attn_b_conv_q, L0_attn_b_conv_k, L0_attn_b_conv_v, L0_attn_b_fir_long, L0_attn_b_fir_short, L0_attn_b_W1, L0_attn_b_b1, L0_attn_b_W2, L0_attn_b_b2, L0_attn_b_log_temp, L0_attn_b_base_bias, L0_attn_b_conv_residual_logit, L0_attn_b_rms_w, L0_attn_b_Wo)
    x = x + _L0_ffn_ref(_layernorm(x, axis=-1), L0_ffn_w_gate, L0_ffn_w_up, L0_ffn_w_down)
    x = x + _L1_attn_a_ref(_layernorm(x, axis=-1), L1_attn_a_W_in, L1_attn_a_conv_w, L1_attn_a_conv_b, L1_attn_a_dt_bias, L1_attn_a_A_log, L1_attn_a_Dp, L1_attn_a_fc_D_w, L1_attn_a_norm_w, L1_attn_a_W_out)
    x = x + _L1_ffn_ref(_layernorm(x, axis=-1), L1_ffn_Wq, L1_ffn_bq, L1_ffn_Wk, L1_ffn_bk, L1_ffn_Wv, L1_ffn_bv, L1_ffn_Wo, L1_ffn_bo, L1_ffn_router_w, L1_ffn_router_b, L1_ffn_W1, L1_ffn_b1, L1_ffn_W2, L1_ffn_b2, L1_ffn_ln1_g, L1_ffn_ln1_b, L1_ffn_ln2_g, L1_ffn_ln2_b)
    x = x + _L1_attn_b_ref(_layernorm(x, axis=-1), L1_attn_b_Wq, L1_attn_b_Wk, L1_attn_b_Wv, L1_attn_b_Wo, L1_attn_b_qn_w, L1_attn_b_kn_w)
    x = x + _L1_ffn_ref(_layernorm(x, axis=-1), L1_ffn_Wq, L1_ffn_bq, L1_ffn_Wk, L1_ffn_bk, L1_ffn_Wv, L1_ffn_bv, L1_ffn_Wo, L1_ffn_bo, L1_ffn_router_w, L1_ffn_router_b, L1_ffn_W1, L1_ffn_b1, L1_ffn_W2, L1_ffn_b2, L1_ffn_ln1_g, L1_ffn_ln1_b, L1_ffn_ln2_g, L1_ffn_ln2_b)
    return x

_drawn_inputs = setup_inputs


def setup_inputs(seed=0):
    import zlib

    import numpy as np

    out = dict(_drawn_inputs(seed))
    spreads = {'L0_attn_b_b1': (0.0, 2.0),
     'L0_attn_b_b2': (0.0, 0.8),
     'L0_attn_b_log_temp': (0.013658997602760792, 0.6),
     'L0_attn_b_conv_residual_logit': (-2.0, 0.6),
     'L0_attn_b_rms_w': (1.0, 0.6),
     'L1_attn_a_A_log': (0.0, 0.8),
     'L1_attn_a_Dp': (1.0, 0.6),
     'L1_attn_a_norm_w': (1.0, 0.6),
     'L1_attn_b_qn_w': (1.0, 0.6),
     'L1_attn_b_kn_w': (1.0, 0.6),
     'L1_ffn_bq': (0.0, 2.0),
     'L1_ffn_bk': (0.0, 2.0),
     'L1_ffn_bv': (0.0, 2.0),
     'L1_ffn_bo': (0.0, 2.0),
     'L1_ffn_b1': (0.0, 2.0),
     'L1_ffn_b2': (0.0, 2.0),
     'L1_ffn_ln1_g': (1.0, 0.6),
     'L1_ffn_ln1_b': (0.0, 2.0),
     'L1_ffn_ln2_g': (1.0, 0.6),
     'L1_ffn_ln2_b': (0.0, 2.0)}
    factors = {'L0_attn_b_Wq': 8.0,
     'L0_attn_b_Wk': 64.0,
     'L0_attn_b_Wv': 49.883,
     'L0_attn_b_Wb': 8.0,
     'L0_attn_b_conv_q': 8.0,
     'L0_attn_b_conv_k': 64.0,
     'L0_attn_b_conv_v': 51.293,
     'L0_attn_b_fir_long': 64.0,
     'L0_attn_b_fir_short': 64.0,
     'L0_attn_b_W1': 64.0,
     'L0_attn_b_W2': 64.0,
     'L0_attn_b_base_bias': 46.531,
     'L0_attn_b_Wo': 43.793,
     'L1_attn_a_W_in': 53.97,
     'L1_attn_a_conv_w': 64.0,
     'L1_attn_a_conv_b': 64.0,
     'L1_attn_a_dt_bias': 8.0,
     'L1_attn_a_fc_D_w': 64.0,
     'L1_attn_a_W_out': 47.842,
     'L1_attn_b_Wq': 64.0,
     'L1_attn_b_Wk': 64.0,
     'L1_attn_b_Wv': 64.0,
     'L1_attn_b_Wo': 64.0,
     'L1_ffn_Wq': 64.0,
     'L1_ffn_Wk': 64.0,
     'L1_ffn_Wv': 64.0,
     'L1_ffn_Wo': 64.0,
     'L1_ffn_router_w': 64.0,
     'L1_ffn_W1': 64.0,
     'L1_ffn_W2': 64.0}
    for name, (base, spread) in spreads.items():
        noise = np.random.default_rng([zlib.crc32(name.encode()), seed]).standard_normal(out[name].shape)
        drawn = base * np.exp(spread * noise) if base else spread * noise
        out[name] = jnp.asarray(drawn.astype(out[name].dtype))
    for name, factor in factors.items():
        out[name] = (out[name] * factor).astype(out[name].dtype)
    return out
```

```python
from contextlib import ExitStack

import concourse.bass as bass
from concourse import mybir

F32 = mybir.dt.float32
BF16 = mybir.dt.bfloat16
I32 = mybir.dt.int32
ALU = mybir.AluOpType
ACT = mybir.ActivationFunctionType
AXX = mybir.AxisListType.X

P = 128
B, L, D = 4, 1024, 128
TPB = L // P
NT = B * TPB
NH, HD = 16, 8
GH = 4
NG = NH // GH
NSTEP = B * NG
NBUF = 4
TERMS = 6
SCALE = float(HD) ** -0.5
NEG = -1.0e30


def ds(start, size):
    return bass.ds(start, size)


def wait(e, sem, value):
    if not (isinstance(value, int) and value <= 0):
        e.wait_ge(sem, value)


def alone(e, core):
    e.sem_inc(core.s_alone, 1)


def batches(e):
    yield 0
    with e.Fori(1, B) as b:
        yield b


def one_ahead(e, first, then):
    first(0)
    first(1)
    then(0)
    with e.Fori(1, B - 1) as b:
        first(b + 1)
        then(b)
    then(B - 1)


class Chain:

    def __init__(self, e, sem):
        self.e, self.sem, self.base, self.n = e, sem, 0, 0

    def __call__(self, ins):
        ins.then_inc(self.sem, 1)
        self.n += 1
        return ins

    def sync(self):
        self.e.wait_ge(self.sem, self.base + self.n)

    def at(self, base):
        self.base, self.n = base, 0


class Core:

    def __init__(self, nc, ctx, ins):
        self.nc, self.ctx, self.ins = nc, ctx, ins
        self.layer_ctx = None
        self.s_w, self.n_w = {}, {}
        self.programs = {"tensor": [], "scalar": [], "vector": [], "gpsimd": [], "sync": []}
        self.x = self.sb("x", [P, NT, D], F32)
        self.ident = self.sb("ident", [P, P], F32)
        self.ident_bf = self.sb("ident_bf", [P, P], BF16)
        self.neghalf = self.sb("neghalf", [P, TPB], F32)
        self.ps = ctx.enter_context(nc.psum_tensor("ps", [P, 8, 512], F32))
        self.s_set = self.kept_sem("constants_set")
        self.s_alone = self.kept_sem("waits_passed")
        self.s_over = self.kept_sem("layer_over")
        self.s_clear = self.kept_sem("semaphores_cleared")
        self.used, self.n_layers = [], 0
        self.prev = None

    def sb(self, name, shape, dt, ctx=None):
        return (ctx or self.layer_ctx or self.ctx).enter_context(self.nc.sbuf_tensor(name, shape, dt))

    def kept_sem(self, name):
        return self.ctx.enter_context(self.nc.semaphore(name))

    def sem(self, name):
        s = self.layer_ctx.enter_context(self.nc.semaphore(name))
        self.used.append(s)
        return s

    def end_layer(self):
        self.layer_ctx.close()
        self.layer_ctx = None
        k, sems, (s_x, n_x) = self.n_layers, self.used, self.prev

        def leave(e):
            e.wait_ge(s_x, n_x)
            e.drain()
            e.sem_inc(self.s_over, 1)

        def clear(e):
            leave(e)
            e.wait_ge(self.s_over, 5 * (k + 1))
            for s in sems:
                e.sem_clear(s)
            e.sem_inc(self.s_clear, 1)

        def enter(e):
            e.wait_ge(self.s_clear, k + 1)
            alone(e, self)

        for name in self.programs:
            self.add(name, clear if name == "gpsimd" else leave)
            self.add(name, enter)
        self.n_layers, self.used = k + 1, []
        self.prev = (self.s_clear, k + 1)

    def begin_layer(self):
        self.layer_ctx = ExitStack()

    def load(self, name, tile, key):
        if name not in self.s_w:
            self.s_w[name], self.n_w[name] = self.kept_sem(name + "_w_loaded"), 0
        sem = self.s_w[name]
        self.n_w[name] += 16
        self.add("sync", lambda e: e.dma_start(tile[:], self.ins[key]).then_inc(sem, 16))

    def dram(self, name, shape, dt):
        return self.nc.dram_tensor(name, shape, dt).ap()

    def add(self, engine, fn):
        self.programs[engine].append(fn)


class Norm:

    def __init__(self, core, name, ctx, banks, eps=1e-5):
        self.c, self.banks, self.eps = core, banks, eps
        self.stats = core.sb(name + "_stats", [P, TPB, 6], F32, ctx)
        self.mv = core.sb(name + "_mv", [P, TPB, 2], F32, ctx)
        self.rstd = core.sb(name + "_rstd", [P, TPB], F32, ctx)
        self.xn = core.sb(name + "_xn", [P, TPB, D], F32, ctx)
        self.xT = core.sb(name + "_xT", [P, L], F32, ctx)
        self.s_stats = core.sem(name + "_stats_done")
        self.s_mv = core.sem(name + "_meanvar_ready")
        self.s_eps = core.sem(name + "_eps_added")
        self.s_rstd = core.sem(name + "_rstd_ready")
        self.s_xn = core.sem(name + "_normed")
        self.s_tp = core.sem(name + "_transposed")
        self.s_xT = core.sem(name + "_xT_ready")

    def vector(self, e, b, transposed=True):
        c = self.c
        for t in range(TPB):
            e.bn_stats(self.stats[:, t, :], c.x[:, ds(b * TPB + t, 1), :].rearrange("p a d -> p (a d)")).then_inc(self.s_stats, 1)
        e.wait_ge(self.s_stats, (b + 1) * TPB)
        wait(e, self.s_rstd, b)
        alone(e, c)
        for t in range(TPB):
            e.bn_aggr(self.mv[:, t, :], self.stats[:, t, :]).then_inc(self.s_mv, 1)
        if transposed:
            wait(e, self.s_tp, b)
        e.wait_ge(self.s_mv, (b + 1) * TPB)
        e.wait_ge(self.s_rstd, b + 1)
        for t in range(TPB):
            e.tensor_scalar(self.xn[:, t, :], c.x[:, ds(b * TPB + t, 1), :].rearrange("p a d -> p (a d)"),
                            self.mv[:, t, 0:1], self.rstd[:, t:t + 1], ALU.subtract, ALU.mult).then_inc(self.s_xn, 1)

    def gpsimd(self, e, b):
        e.wait_ge(self.s_mv, (b + 1) * TPB)
        wait(e, self.s_xn, b * TPB)
        alone(e, self.c)
        e.tensor_scalar(self.rstd[:, :], self.mv[:, :, 1], self.eps, None, ALU.add).then_inc(self.s_eps, 1)
        e.wait_ge(self.s_eps, b + 1)
        e.tensor_tensor(self.rstd[:, :], self.rstd[:, :], self.c.neghalf[:, :], ALU.pow).then_inc(self.s_rstd, 1)

    def tensor(self, e, b):
        e.wait_ge(self.s_xn, (b + 1) * TPB)
        wait(e, self.s_xT, 2 * b)
        for t in range(TPB):
            m = e.transpose(self.c.ps[:, self.banks[t // 4], (t % 4) * P:(t % 4 + 1) * P], self.xn[:, t, :], self.c.ident[:, :])
        m.then_inc(self.s_tp, 1)

    def scalar(self, e, b):
        e.wait_ge(self.s_tp, b + 1)
        for h in range(2):
            e.activation(self.xT[:, h * 512:(h + 1) * 512], self.c.ps[:, self.banks[h], :], ACT.Copy).then_inc(self.s_xT, 1)


def ffn(core, name, wg, wu, wd, scale, s_w, n_w):
    c, HC = core, 3
    with ExitStack() as ctx:
        norm = Norm(core, name, ctx, (0, 1))
        h = core.sb(name + "_h", [P, HC, L], F32, ctx)
        sil = core.sb(name + "_silu", [P, L], F32, ctx)
        up = core.sb(name + "_up", [P, L], F32, ctx)
    prev = core.prev
    s_gate = core.sem(name + "_gate_ready")
    s_up = core.sem(name + "_up_ready")
    s_sil = core.sem(name + "_silu_ready")
    s_upc = core.sem(name + "_up_copied")
    s_h = core.sem(name + "_hidden_ready")
    s_y = core.sem(name + "_down_ready")
    s_x = core.sem(name + "_residual_ready")
    GB, UB, YB = (2, 3), (4, 5), (6, 7)

    def tensor(e):
        e.wait_ge(*prev)
        e.wait_ge(s_w, n_w)
        for b in batches(e):
            norm.tensor(e, b)
            e.wait_ge(norm.s_xT, 2 * (b + 1))
            for j in range(HC):
                wait(e, s_sil, HC * b + j)
                for k in range(2):
                    m = e.matmul(c.ps[:, GB[k], :], wg[:, j * P:(j + 1) * P], norm.xT[:, k * 512:(k + 1) * 512], start=True, stop=True)
                m.then_inc(s_gate, 1)
                wait(e, s_upc, HC * b + j)
                for k in range(2):
                    m = e.matmul(c.ps[:, UB[k], :], wu[:, j * P:(j + 1) * P], norm.xT[:, k * 512:(k + 1) * 512], start=True, stop=True)
                m.then_inc(s_up, 1)
            e.wait_ge(s_h, HC * (b + 1))
            wait(e, s_x, b)
            for t in range(TPB):
                for j in range(HC):
                    m = e.matmul(c.ps[:, YB[t // 4], (t % 4) * P:(t % 4 + 1) * P], h[:, j, t * P:(t + 1) * P],
                                 wd[:, j, :], start=(j == 0), stop=(j == HC - 1))
            m.then_inc(s_y, 1)

    def scalar(e):
        e.wait_ge(*prev)
        for b in batches(e):
            wait(e, s_up, HC * b)
            norm.scalar(e, b)
            for j in range(HC):
                e.wait_ge(s_gate, HC * b + j + 1)
                wait(e, s_h, HC * b + j)
                e.activation(sil[:, :], c.ps[:, GB[0]:GB[0] + 2, :].rearrange("p a n -> p (a n)"), ACT.Silu, scale=scale).then_inc(s_sil, 1)
                e.wait_ge(s_up, HC * b + j + 1)
                e.activation(up[:, :], c.ps[:, UB[0]:UB[0] + 2, :].rearrange("p a n -> p (a n)"), ACT.Copy, scale=scale).then_inc(s_upc, 1)

    def vector(e):
        e.wait_ge(*prev)

        def hidden_and_residual(b):
            for j in range(HC):
                e.wait_ge(s_sil, HC * b + j + 1)
                e.wait_ge(s_upc, HC * b + j + 1)
                if j == 0:
                    wait(e, s_y, b)
                e.tensor_tensor(h[:, j, :], sil[:, :], up[:, :], ALU.mult).then_inc(s_h, 1)
            e.wait_ge(s_y, b + 1)
            xb = c.x[:, ds(b * TPB, TPB), :].rearrange("p t d -> p (t d)")
            e.scalar_tensor_tensor(out=xb, in0=c.ps[:, YB[0]:YB[0] + 2, :].rearrange("p a n -> p (a n)"), scalar=scale,
                                   in1=xb, op0=ALU.mult, op1=ALU.add).then_inc(s_x, 1)

        one_ahead(e, lambda b: norm.vector(e, b), hidden_and_residual)

    def gpsimd(e):
        e.wait_ge(*prev)
        for b in batches(e):
            norm.gpsimd(e, b)

    core.add("tensor", tensor)
    core.add("scalar", scalar)
    core.add("vector", vector)
    core.add("gpsimd", gpsimd)
    core.prev = (s_x, B)


Q_PARTS = (0, 0, 0, 1, 1, 2)
K_PARTS = (0, 1, 2, 0, 1, 0)
ROWS = TERMS * HD
BIAS_ROWS = 27
QT = TPB


class Step:

    def __init__(self, u, k):
        self.u, self.k = u, k
        self.v = k if isinstance(u, int) else u * NBUF + k
        self.rounds = k // NBUF if isinstance(u, int) else u + k // NBUF

    def __add__(self, n):
        return Step(self.u, self.k + n)

    def __sub__(self, n):
        return Step(self.u, self.k - n)


def steps(e):
    yield Step(0, 0)
    with e.Fori(0, (NSTEP - 4) // NBUF) as u:
        for r in range(NBUF):
            yield Step(u, 1 + r)
    for k in range(NSTEP - 3, NSTEP):
        yield Step(0, k)


def split(e, chain, src, parts, rest, core):
    chain(e.tensor_copy(parts[0], src))
    chain.sync()
    chain(e.tensor_tensor(rest, src, parts[0], ALU.subtract))
    chain.sync()
    alone(e, core)
    chain(e.tensor_copy(parts[1], rest))
    chain.sync()
    return chain(e.tensor_tensor(parts[2], rest, parts[1], ALU.subtract))


def attention(core, name, w, bias=None, rms=None, causal=False, v_bias=None):
    c = core
    alibi = causal
    FILL = BIAS_ROWS if alibi else 17
    KMAX = ROWS + FILL
    KEXP = KMAX + 3
    prev = core.prev
    qd = c.dram(name + "_q_parts_dram", [3, NSTEP, GH, HD, L], BF16)
    kd = c.dram(name + "_k_parts_dram", [3, NSTEP, GH, HD, L], BF16)
    md = c.dram(name + "_max_parts_dram", [2, 4, GH * QT, 3, 32], BF16)

    ctx = ExitStack()
    o = c.sb(name + "_o", [P, NSTEP, QT, GH * HD], F32, ctx)
    v = c.sb(name + "_v", [P, NSTEP, QT, GH * HD], F32, ctx)

    actx = ExitStack()
    norm = Norm(core, name, actx, (0, 1))
    qf = [c.sb(f"{name}_{n}_full", [P, L], F32, actx) for n in "qk"]
    rest = [c.sb(f"{name}_{n}_rest", [P, L], F32, actx) for n in "qk"]
    parts = [c.sb(f"{name}_{n}_parts", [P, 3, L], BF16, actx) for n in "qk"]
    if rms:
        sq = [c.sb(f"{name}_{n}_squares", [P, L], F32, actx) for n in "qk"]
        mean = [c.sb(f"{name}_{n}_mean", [P, L], F32, actx) for n in "qk"]
        s_ln = [c.sem(f"{name}_{n}_logarithm_ready") for n in "qk"]
        s_sq = [c.sem(f"{name}_{n}_squared") for n in "qk"]
        s_ms = [c.sem(f"{name}_{n}_sums_ready") for n in "qk"]
        s_mean = [c.sem(f"{name}_{n}_mean_copied") for n in "qk"]
        s_rs = [c.sem(f"{name}_{n}_rsqrt_ready") for n in "qk"]
        s_qn = [c.sem(f"{name}_{n}_rmsnormed") for n in "qk"]
    actx.close()
    s_proj = [c.sem(f"{name}_{n}_projected") for n in "qkv"]
    s_qf = [c.sem(f"{name}_{n}_copied") for n in "qk"]
    s_v = c.sem(name + "_v_copied")
    s_split = [c.sem(f"{name}_{n}_split") for n in "qk"]
    s_pw = [c.sem(f"{name}_{n}_parts_written") for n in "qk"]
    SPLIT = 4
    s_free = s_mean if rms else s_qf
    PB = ((2, 3), (4, 5))

    def proj_tensor(e):
        e.wait_ge(*prev)
        e.wait_ge(c.s_w[name], c.n_w[name])
        for b in batches(e):
            norm.tensor(e, b)
            e.wait_ge(norm.s_xT, 2 * (b + 1))
            for n in range(2):
                wait(e, s_free[n], b)
                for k in range(2):
                    m = e.matmul(c.ps[:, PB[n][k], :], w[:, n * P:(n + 1) * P], norm.xT[:, k * 512:(k + 1) * 512], start=True, stop=True)
                m.then_inc(s_proj[n], 1)
            wait(e, s_v, 2 * b)
            for t in range(QT):
                m = e.matmul(c.ps[:, 6 + t // 4, (t % 4) * P:(t % 4 + 1) * P], norm.xT[:, t * P:(t + 1) * P], w[:, 2 * P:3 * P], start=True, stop=True)
            m.then_inc(s_proj[2], 1)
            if rms:
                for n in range(2):
                    e.wait_ge(s_sq[n], b + 1)
                    for k in range(2):
                        m = e.matmul(c.ps[:, PB[n][k], :], c.head_ones[:, :], sq[n][:, k * 512:(k + 1) * 512], start=True, stop=True)
                    m.then_inc(s_ms[n], 1)

    def flat(bank):
        return c.ps[:, bank:bank + 2, :].rearrange("p a n -> p (a n)")

    def proj_scalar(e):
        e.wait_ge(*prev)
        for b in batches(e):
            wait(e, s_proj[2], b)
            norm.scalar(e, b)
            for n in range(2):
                e.wait_ge(s_proj[n], b + 1)
                wait(e, s_split[n], SPLIT * b)
                if bias is not None:
                    e.activation(qf[n][:, :], flat(PB[n][0]), ACT.Identity, bias=bias[:, n:n + 1]).then_inc(s_qf[n], 1)
                elif rms:
                    e.activation(qf[n][:, :], flat(PB[n][0]), ACT.Copy).then_inc(s_qf[n], 1)
                    wait(e, s_ms[n], b)
                    e.activation(sq[n][:, :], flat(PB[n][0]), ACT.Square).then_inc(s_sq[n], 1)
                else:
                    e.activation(qf[n][:, :], flat(PB[n][0]), ACT.Copy).then_inc(s_qf[n], 1)
            e.wait_ge(s_proj[2], b + 1)
            alone(e, c)
            for k in range(2):
                out = v[:, ds(b * NG, NG), 4 * k:4 * k + 4, :].rearrange("p g t d -> p t g d")
                src = c.ps[:, 6 + k, :].rearrange("p (t g d) -> p t g d", t=4, g=NG)
                if v_bias is None:
                    e.activation(out, src, ACT.Copy).then_inc(s_v, 1)
            if rms:
                for n in range(2):
                    e.wait_ge(s_ms[n], b + 1)
                    wait(e, s_qn[n], b)
                    e.activation(mean[n][:, :], flat(PB[n][0]), ACT.Copy, scale=1.0 / HD, bias=rms[1]).then_inc(s_mean[n], 1)
                for n in range(2):
                    e.wait_ge(s_mean[n], b + 1)
                    alone(e, c)
                    e.activation(mean[n][:, :], mean[n][:, :], ACT.Ln).then_inc(s_ln[n], 1)
                for n in range(2):
                    e.wait_ge(s_ln[n], b + 1)
                    alone(e, c)
                    e.activation(mean[n][:, :], mean[n][:, :], ACT.Exp, scale=-0.5).then_inc(s_rs[n], 1)

    def rms_scale(e, b, n):
        e.wait_ge(s_rs[n], b + 1)
        e.wait_ge(s_qf[n], b + 1)
        wait(e, s_split[n], SPLIT * b)
        e.scalar_tensor_tensor(out=rest[n][:, :], in0=qf[n][:, :], scalar=rms[0][:, n:n + 1], in1=mean[n][:, :],
                               op0=ALU.mult, op1=ALU.mult).then_inc(s_qn[n], 1)
        e.wait_ge(s_qn[n], b + 1)

    def split_qk(e, b, n, chain):
        if not rms:
            e.wait_ge(s_qf[n], b + 1)
        wait(e, s_pw[n], 16 * b)
        alone(e, c)
        chain.at(SPLIT * b)
        src = rest[n] if rms else qf[n]
        spare = qf[n] if rms else rest[n]
        split(e, chain, src[:, :], [parts[n][:, i, :] for i in range(3)], spare[:, :], c)

    def v_out_vector(e, b):
        e.wait_ge(s_proj[2], b + 1)
        alone(e, c)
        for t in range(QT):
            out = v[:, ds(b * NG, NG), t, :]
            src = c.ps[:, 6 + t // 4, (t % 4) * P:(t % 4 + 1) * P].rearrange("p (g d) -> p g d", g=NG)
            m = e.tensor_tensor(out, src, v_bias.rearrange("p (g d) -> p g d", g=NG), ALU.add)
        m.then_inc(s_v, 2)

    def proj_vector(e):
        e.wait_ge(*prev)
        e.wait_ge(c.s_w[name], c.n_w[name])
        ch = [Chain(e, s_split[0]), Chain(e, s_split[1])]

        def scale_and_split(b):
            if rms:
                rms_scale(e, b, 0)
                rms_scale(e, b, 1)
            if v_bias is not None:
                v_out_vector(e, b)
            split_qk(e, b, 0, ch[0])
            if rms:
                split_qk(e, b, 1, ch[1])

        one_ahead(e, lambda b: norm.vector(e, b), scale_and_split)

    def proj_gpsimd(e):
        e.wait_ge(*prev)
        ch = Chain(e, s_split[1])
        one_ahead(e, lambda b: norm.gpsimd(e, b), lambda b: rms or split_qk(e, b, 1, ch))

    def proj_sync(e):
        e.wait_ge(*prev)
        for b in batches(e):
            for n, dst in ((0, qd), (1, kd)):
                e.wait_ge(s_split[n], SPLIT * (b + 1))
                alone(e, c)
                e.dma_start(dst[:, ds(b * NG, NG)].rearrange("r g j d t -> (g j d) r t"), parts[n][:, :, :]).then_inc(s_pw[n], 16)

    bctx = ExitStack()
    qs = c.sb(name + "_q_stack", [P, NBUF, GH, L], BF16, bctx)
    ks = c.sb(name + "_k_stack", [P, NBUF, GH, L], BF16, bctx)
    pr = c.sb(name + "_probs", [P, 2, GH, L], F32, bctx)
    vs = c.sb(name + "_v_stage", [P, 2, QT, GH, 32], F32, bctx)
    acc = c.sb(name + "_acc", [P, L], F32, bctx)
    mx = c.sb(name + "_max_pieces", [P, GH, QT, 2], F32, bctx)
    nm = c.sb(name + "_negmax", [P, GH * QT], F32, bctx)
    nmt = c.sb(name + "_negmax_t", [P, 32], F32, bctx)
    nmr = c.sb(name + "_negmax_rest", [P, 32], F32, bctx)
    nmp = c.sb(name + "_negmax_parts", [P, 3, 32], BF16, bctx)
    rec = c.sb(name + "_recip", [P, QT, GH], F32, bctx)
    bctx.close()
    s_ld = [c.sem(f"{name}_qk_loaded{i}") for i in range(NBUF)]
    s_row = c.sem(name + "_bias_rows_loaded")
    s_st = c.sem(name + "_scoresT_ready")
    s_exp = c.sem(name + "_exp_done")
    s_pv = c.sem(name + "_pv_done")
    s_acc = c.sem(name + "_acc_copied")
    s_ot = c.sem(name + "_outputs_transposed")
    s_on = c.sem(name + "_outputs_normed")
    s_s = c.sem(name + "_scores_ready")
    s_mx = c.sem(name + "_max_taken")
    s_mch = c.sem(name + "_max_steps")
    s_mw = c.sem(name + "_max_written")
    s_mr = c.sem(name + "_max_rows_ready")
    s_vs = c.sem(name + "_v_staged")
    s_rec = c.sem(name + "_recip_ready")
    s_fill = c.sem(name + "_stage_filled")
    MCH = 6
    AHEAD = 2
    LDQ = 16 * (2 * TERMS + (1 if alibi else 0))
    NROW = 2 if alibi else 3
    s_clr = c.sem(name + "_pieces_cleared")

    pieces = []
    for qt in range(QT):
        for j in range(GH):
            end = (qt + 1) * P if causal else L
            for half in range(2):
                if half * 512 < end:
                    pieces.append((j, qt, half, half * 512, min(half * 512 + 512, end)))
    NPC = len(pieces)
    NTILE = QT * GH

    def psum_s(half, n):
        return c.ps[:, 4 + half, 0:n]

    def max_piece_tensor(e, s, buf, n):
        j, qt, half, k0, k1 = pieces[n]
        if n == 0:
            e.wait_ge(s_ld[buf], LDQ * (s.rounds + 1))
        g = NPC * s.v + n
        wait(e, s_mx, g - 1)
        diag = causal and (qt * P >= k0 and qt * P < k1)
        m = e.matmul(psum_s(g_half(n), k1 - k0), qs[0:KMAX, buf, j, qt * P:(qt + 1) * P], ks[0:KMAX, buf, j, k0:k1],
                     start=True, stop=not diag)
        if diag:
            m = e.matmul(c.ps[:, 4 + g_half(n), qt * P - k0:qt * P - k0 + P], c.ident_bf[:, :], c.mask_q[:, :], start=False, stop=True)
        m.then_inc(s_s, 1)

    def g_half(n):
        return n % 2

    assert NPC % 2 == 0

    def tile_tensor(e, s, buf, n):
        kt, j = n // GH, n % GH
        lo = kt * P if causal else 0
        if n == 0:
            e.wait_ge(s_mr, 48 * (s.v + 1))
        wait(e, s_exp, NTILE * s.v + n - 1)
        base = 2 * (n % 2)
        spans = [(max(lo, 0), 512), (max(lo, 512), L)] if lo < 512 else [(lo, L)]
        for a, z in spans:
            bank = base + a // 512
            diag = causal and a == lo
            m = e.matmul(c.ps[:, bank, a % 512:a % 512 + z - a], ks[0:KEXP, buf, j, kt * P:(kt + 1) * P], qs[0:KEXP, buf, j, a:z],
                         start=True, stop=not diag)
            if diag:
                m = e.matmul(c.ps[:, bank, a % 512:a % 512 + P], c.ident_bf[:, :], c.mask_k[:, :], start=False, stop=True)
        m.then_inc(s_st, 1)

    def pv_tensor(e, s, kt, par, halves=(0, 1)):
        if 0 in halves:
            e.wait_ge(s_exp, NTILE * s.v + GH * (kt + 1))
        if kt == 0:
            e.wait_ge(s_vs, s.v + 1)
            wait(e, s_on, s.v)
        lo = kt * P if causal else 0
        for half in halves:
            a, z = max(lo, half * 512), half * 512 + 512
            if a >= z:
                continue
            last = (z - 1) // P if causal else QT - 1
            for j in range(GH):
                m = e.matmul(c.ps[32 * j:32 * j + 32, 6 + half, a % 512:a % 512 + z - a], vs[:, par, kt, j, :], pr[:, kt % 2, j, a:z],
                             start=(kt == 0), stop=(kt == last), skip_group_check=True)
        if 1 in halves:
            m.then_inc(s_pv, 1)

    def out_tensor(e, s):
        e.wait_ge(s_acc, s.v + 1)
        for t in range(QT):
            m = e.transpose(c.ps[:, 6 + t // 4, (t % 4) * P:(t % 4 + 1) * P], acc[:, t * P:(t + 1) * P], c.ident[:, :])
        m.then_inc(s_ot, 1)

    def step_tensor(e, s, first, ahead):
        r = s.k
        done = 0
        for n in range(NTILE):
            tile_tensor(e, s, r % NBUF, n)
            if not first and n in (1, 3):
                pv_tensor(e, s - 1, QT - 1, (r + 1) % 2, (n // 2,))
            if not first and n == GH + 1:
                out_tensor(e, s - 1)
            if n == 2 * GH - 1:
                pv_tensor(e, s, 0, r % 2)
            if n >= 2 * GH and n % 2:
                pv_tensor(e, s, n // GH - 1, r % 2, (n % GH // 2,))
            if ahead:
                until = (2 if first else 1) * NPC * (n + 1) // NTILE
                while done < until:
                    k = 1 + done // NPC if first else AHEAD
                    max_piece_tensor(e, s + k, (r + k) % NBUF, done % NPC)
                    done += 1

    def step_scalar(e, s, first):
        for n in range(NTILE):
            kt, j = n // GH, n % GH
            lo = kt * P if causal else 0
            e.wait_ge(s_st, NTILE * s.v + n + 1)
            wait(e, s_pv, QT * s.v + kt - 1)
            alone(e, c)
            src = c.ps[:, 2 * (n % 2):2 * (n % 2) + 2, :].rearrange("p a n -> p (a n)")[:, lo:L]
            e.activation(pr[:, kt % 2, j, lo:L], src, ACT.Exp, scale=SCALE).then_inc(s_exp, 1)
            if n == GH - 1 and not first:
                copy_acc(e, s - 1)

    def copy_acc(e, s):
        e.wait_ge(s_pv, QT * (s.v + 1))
        wait(e, s_ot, s.v)
        alone(e, c)
        e.activation(acc[:, :], flat(6), ACT.Copy).then_inc(s_acc, 1)

    def max_vector(e, s, n):
        j, qt, half, k0, k1 = pieces[n]
        e.wait_ge(s_s, NPC * s.v + n + 1)
        if n == 0:
            wait(e, s_mch, MCH * s.v)
            alone(e, c)
        e.tensor_reduce(mx[:, j, qt, half:half + 1], psum_s(g_half(n), k1 - k0), AXX, ALU.max).then_inc(s_mx, 1)

    def max_end_vector(e, s, chain):
        chain.at(MCH * s.v)
        e.wait_ge(s_mx, NPC * (s.v + 1))
        chain(e.tensor_reduce(nm[:, :], mx[:, :, :, :].rearrange("p j t h -> p (j t) h"), AXX, ALU.max, negate=True))
        chain.sync()
        chain(e.transpose(nmt[:, :], nm[:, :]))
        chain.sync()
        wait(e, s_mw, 16 * s.v)
        alone(e, c)
        split(e, chain, nmt[:, :], [nmp[:, i, :] for i in range(3)], nmr[:, :], c)

    def out_vector(e, s):
        e.wait_ge(s_ot, s.v + 1)
        src = c.ps[:, 6:8, :].rearrange("p a (t j d) -> p (a t) j d", t=4, j=GH)
        e.reciprocal(rec[:, :, :], src[:, :, :, HD]).then_inc(s_rec, 1)
        e.wait_ge(s_rec, s.v + 1)
        for k in range(2):
            dst = o[:, ds(s.v, 1), 4 * k:4 * k + 4, :].rearrange("p a t (j d) -> p (a t) j d", j=GH)
            m = e.tensor_tensor(dst, src[:, 4 * k:4 * k + 4, :, 0:HD], rec[:, 4 * k:4 * k + 4, :].unsqueeze(3).to_broadcast([P, 4, GH, HD]), ALU.mult)
        m.then_inc(s_on, 1)

    def step_vector(e, s, chain, first, ahead):
        for n in range(NPC if ahead else 0):
            max_vector(e, s + AHEAD, n)
            if n == NPC * 6 // NTILE and not first:
                out_vector(e, s - 1)
        if ahead:
            max_end_vector(e, s + AHEAD, chain)
        elif not first:
            out_vector(e, s - 1)

    def stage_v(e, s, par):
        wait(e, s_pv, QT * (s - 1))
        alone(e, c)
        e.tensor_copy(vs[:, par, :, :, 0:HD], v[:, ds(s, 1), :, :].rearrange("p a t (j d) -> p (a t) j d", j=GH)).then_inc(s_vs, 1)

    def load(e, s):
        buf = s.k % NBUF
        for dst, src, order in ((qs, qd, Q_PARTS), (ks, kd, K_PARTS)):
            for i, p in enumerate(order):
                e.dma_start(dst[i * HD:(i + 1) * HD, buf, :, :], src[p, ds(s.v, 1)].rearrange("a j d t -> d (a j) t")).then_inc(s_ld[buf], 16)
        if alibi:
            e.dma_start(ks[ROWS:ROWS + BIAS_ROWS, buf, :, :], c.ins["bias_k"][ds(s.v, 1)].rearrange("a r j t -> (a r) j t")).then_inc(s_ld[buf], 16)

    def max_rows(e, s):
        half = s.k % 2
        e.wait_ge(s_mch, MCH * (s.v + 1))
        alone(e, c)
        wait(e, s_mr, 48 * (s.v - 1) if not isinstance(s.v, int) or s.v > 1 else 0)
        alone(e, c)
        e.dma_start(md[half].rearrange("i c r u -> (i c) r u"), nmp[:, :, :]).then_inc(s_mw, 16)
        e.wait_ge(s_mw, 16 * (s.v + 1))
        alone(e, c)
        for r in range(3):
            e.dma_start(qs[KMAX + r:KMAX + r + 1, s.k % NBUF, :, :].rearrange("r j (t i u) -> r (j t) i u", t=QT, i=4),
                        md[half, :, :, r:r + 1, :].rearrange("i c r u -> r c i u")).then_inc(s_mr, 16)

    def attn_tensor(e):
        e.wait_ge(s_v, 2 * B)
        e.wait_ge(s_free[0], B)
        e.wait_ge(s_free[1], B)
        e.wait_ge(s_row, 16 * NROW * NBUF)
        e.wait_ge(s_fill, 2)
        for n in range(NPC):
            max_piece_tensor(e, Step(0, 0), 0, n)
        for s in steps(e):
            step_tensor(e, s, is_first(s), in_time(s))
        pv_tensor(e, Step(0, NSTEP - 1), QT - 1, (NSTEP - 1) % 2)
        out_tensor(e, Step(0, NSTEP - 1))

    def is_first(s):
        return isinstance(s.v, int) and s.v == 0

    def in_time(s):
        return not isinstance(s.v, int) or s.v + AHEAD < NSTEP

    def attn_scalar(e):
        for s in steps(e):
            step_scalar(e, s, is_first(s))
        copy_acc(e, Step(0, NSTEP - 1))

    def attn_vector(e):
        chain = Chain(e, s_mch)
        e.wait_ge(s_fill, 2)
        e.memset(mx[:, :, :, :], -3.0e38).then_inc(s_clr, 1)
        e.wait_ge(s_clr, 1)
        for k in range(2):
            for n in range(NPC):
                max_vector(e, Step(0, k), n)
            max_end_vector(e, Step(0, k), chain)
        for s in steps(e):
            step_vector(e, s, chain, is_first(s), in_time(s))
        out_vector(e, Step(0, NSTEP - 1))

    def attn_gpsimd(e):
        e.wait_ge(s_v, 2 * B)
        e.wait_ge(s_proj[2], B)
        e.wait_ge(s_pw[0], 16 * B)
        e.wait_ge(s_pw[1], 16 * B)
        e.memset(vs[:, :, :, :, :], 0.0).then_inc(s_fill, 1)
        e.wait_ge(s_fill, 1)
        e.memset(vs[:, :, :, :, HD:HD + 1], 1.0).then_inc(s_fill, 1)
        e.wait_ge(s_fill, 2)
        for s in range(2):
            stage_v(e, s, s)
        with e.Fori(1, NSTEP // 2) as u:
            stage_v(e, u * 2, 0)
            stage_v(e, u * 2 + 1, 1)

    def attn_sync(e):
        e.wait_ge(s_pw[0], 16 * B)
        e.wait_ge(s_pw[1], 16 * B)
        e.wait_ge(s_proj[2], B)
        e.wait_ge(s_v, 2 * B)
        for buf in range(NBUF):
            e.dma_start(ks[KMAX:KEXP, buf, :, :], c.ins["ones3"]).then_inc(s_row, 16)
            if alibi:
                e.dma_start(qs[ROWS:KMAX, buf, :, :], c.ins["bias_q"]).then_inc(s_row, 16)
            else:
                e.dma_start(qs[ROWS:KMAX, buf, :, :], c.ins["zero_rows"]).then_inc(s_row, 16)
                e.dma_start(ks[ROWS:KMAX, buf, :, :], c.ins["zero_rows"]).then_inc(s_row, 16)
        for k in range(NBUF):
            load(e, Step(0, k))
        for k in range(2):
            max_rows(e, Step(0, k))
        for s in steps(e):
            if not isinstance(s.v, int):
                e.wait_ge(s_st, NTILE * s.v)
                alone(e, c)
                load(e, s + (NBUF - 1))
            if in_time(s):
                max_rows(e, s + AHEAD)

    core.add("tensor", proj_tensor)
    core.add("scalar", proj_scalar)
    core.add("vector", proj_vector)
    core.add("gpsimd", proj_gpsimd)
    core.add("sync", proj_sync)
    core.add("tensor", attn_tensor)
    core.add("scalar", attn_scalar)
    core.add("vector", attn_vector)
    core.add("gpsimd", attn_gpsimd)
    core.add("sync", attn_sync)
    return ctx, o, (s_on, NSTEP), s_acc


def out_proj(core, name, o, o_ready, octx, wo):
    c = core
    with ExitStack() as ctx:
        on = c.sb(name + "_o_batch", [P, QT, NG, GH * HD], F32, ctx)
        oT = c.sb(name + "_oT", [P, L], F32, ctx)
    octx.close()
    s_on = c.sem(name + "_o_staged")
    s_tp = c.sem(name + "_oT_transposed")
    s_oT = c.sem(name + "_oT_ready")
    s_y = c.sem(name + "_projected_out")
    s_x = c.sem(name + "_residual_ready")

    def gpsimd(e):
        e.wait_ge(*o_ready)
        for b in batches(e):
            wait(e, s_tp, b)
            alone(e, c)
            e.tensor_copy(on[:, :, :, :].rearrange("p t g d -> p g t d"), o[:, ds(b * NG, NG), :, :]).then_inc(s_on, 1)

    def tensor(e):
        e.wait_ge(*o_ready)
        for b in batches(e):
            e.wait_ge(s_on, b + 1)
            wait(e, s_oT, 2 * b)
            for t in range(QT):
                m = e.transpose(c.ps[:, t // 4, (t % 4) * P:(t % 4 + 1) * P], on[:, t, :, :].rearrange("p g d -> p (g d)"), c.ident[:, :])
            m.then_inc(s_tp, 1)
            e.wait_ge(s_oT, 2 * (b + 1))
            wait(e, s_x, b)
            for t in range(QT):
                m = e.matmul(c.ps[:, 2 + t // 4, (t % 4) * P:(t % 4 + 1) * P], oT[:, t * P:(t + 1) * P], wo, start=True, stop=True)
            m.then_inc(s_y, 1)

    def scalar(e):
        e.wait_ge(*o_ready)
        for b in batches(e):
            e.wait_ge(s_tp, b + 1)
            wait(e, s_y, b)
            alone(e, c)
            for k in range(2):
                e.activation(oT[:, k * 512:(k + 1) * 512], c.ps[:, k, :], ACT.Copy).then_inc(s_oT, 1)

    def vector(e):
        e.wait_ge(*o_ready)
        for b in batches(e):
            e.wait_ge(s_y, b + 1)
            xb = c.x[:, ds(b * TPB, TPB), :].rearrange("p t d -> p (t d)")
            e.scalar_tensor_tensor(out=xb, in0=c.ps[:, 2:4, :].rearrange("p a n -> p (a n)"), scalar=1.0,
                                   in1=xb, op0=ALU.mult, op1=ALU.add).then_inc(s_x, 1)

    for n, f in (("gpsimd", gpsimd), ("tensor", tensor), ("scalar", scalar), ("vector", vector)):
        core.add(n, f)
    core.prev = (s_x, B)


def load_weights(core, name, key):
    n = core.ins[key].shape[1]
    w = core.sb(name + "_w", [P, n], F32)
    core.load(name, w, key)
    return w


def attn_alibi(core, name):
    w = load_weights(core, name, "w_alibi")
    core.mask_q = core.sb("mask_q", [P, P], BF16)
    core.mask_k = core.sb("mask_k", [P, P], BF16)
    core.load(name, core.mask_q, "mask_q")
    core.load(name, core.mask_k, "mask_k")
    ctx, o, ready, _ = attention(core, name, w, causal=True)
    out_proj(core, name, o, ready, ctx, w[:, 3 * P:4 * P])


def attn_rms(core, name):
    w = load_weights(core, name, "w_rms")
    core.head_ones = w[:, 4 * P:5 * P]
    ctx, o, ready, _ = attention(core, name, w, rms=(w[:, 5 * P:5 * P + 2], 1.1920929e-07))
    out_proj(core, name, o, ready, ctx, w[:, 3 * P:4 * P])


def attn_moe(core, name):
    w = load_weights(core, name, "w_moe")
    w1 = core.sb(name + "_w1", [P, NE, NF * P], F32)
    w2 = core.sb(name + "_w2", [P, NE, NF, D], F32)
    rows = core.sb(name + "_rows", [P, 7 + NE, D], F32)
    for tile, key in ((w1, "moe_w1"), (w2, "moe_w2"), (rows, "moe_rows")):
        core.load(name, tile, key)
    ctx, o, ready, _ = attention(core, name, w, bias=w[:, 4 * P:4 * P + 2], v_bias=rows[:, VB, :])
    moe(core, name, o, ready, ctx, w, w1, w2, rows)


def layout_attn(f, r, np):
    bf = mybir.dt.np(BF16)

    def parts(a):
        a = a.astype(np.float64)
        out = []
        for _ in range(3):
            p = a.astype(np.float32).astype(bf)
            out.append(p)
            a = a - p.astype(np.float64)
        return out

    r["w_alibi"] = np.concatenate([f("L0_attn_a_" + n + "_w") for n in "qkvo"], 1)
    ones = np.kron(np.eye(NH), np.ones((HD, HD))).astype(np.float32)
    col = lambda n: np.tile(f(n), NH)[:, None]
    r["w_rms"] = np.concatenate([f("L1_attn_b_W" + n).T for n in "qkvo"] + [ones, col("L1_attn_b_qn_w"), col("L1_attn_b_kn_w")], 1)
    r["zero_rows"] = np.zeros((17, GH, L), bf)
    r["ones3"] = np.ones((3, GH, L), bf)
    q = np.arange(P)
    r["mask_q"] = np.where(q[None, :] > q[:, None], NEG, 0.0).astype(bf)
    r["mask_k"] = np.ascontiguousarray(r["mask_q"].T)
    ratio = 2.0 ** (-8.0 / NH)
    slope = np.array([np.float32(ratio ** (i + 1)) for i in range(NH)], np.float64) / SCALE
    tok = np.arange(L)
    places = np.concatenate([(tok[None, :] // P == np.arange(QT)[:, None]), (tok % P)[None, :]], 0).astype(bf)
    r["bias_q"] = np.ascontiguousarray(np.broadcast_to(np.tile(places, (3, 1))[:, None, :], (BIAS_ROWS, GH, L)))
    rows = np.zeros((NH, 9, L))
    rows[:, 0:QT] = -slope[:, None, None] * (np.arange(QT)[None, :, None] * P - tok[None, None, :])
    rows[:, QT] = -slope[:, None]
    k3 = np.stack(parts(rows), 1).reshape(NG, GH, BIAS_ROWS, L).transpose(0, 2, 1, 3)
    r["bias_k"] = np.ascontiguousarray(np.tile(k3, (B, 1, 1, 1)))


DH, DK = 4, 32
CS = 32
NCH = L // CS
CT = P // CS
LONG, SHORT, QTAPS = 64, 5, 4
POOL_TAPS = 46
NLV = 4
DW_P = 0
DW_ONES = 4 * P
DW_W1 = DW_ONES + P
DW_O = DW_W1 + P
DW_W2 = DW_O + P
DW_B1 = DW_W2 + 4
DW_CV = DW_B1 + 1
DW_FS = DW_CV + 3 * QTAPS
DW_FL = DW_FS + SHORT
DW_HM = DW_FL + LONG
DW_ROWS = DW_HM + DH
DM_UP, DM_IN, DM_ID, DM_BD, DM_M = 0, P, 2 * P, 3 * P, 4 * P
DM_C = DM_M + (NLV + 1) * P


def delta(core, name):
    c = core
    w = load_weights(core, name, "w_delta")
    mk = core.sb("delta_masks", [P, core.ins["delta_masks"].shape[1]], F32)
    w1s = core.sb("delta_w1s", [DH * 16, DH, P], F32)
    core.load(name, mk, "delta_masks")
    core.load(name, w1s, "delta_w1s")
    s_w, n_w = core.s_w[name], core.n_w[name]
    prev = core.prev
    H4 = lambda ap, n=P: ap.unsqueeze(1).to_broadcast([P, DH, n])
    with ExitStack() as ctx:
        norm = Norm(core, name, ctx, (0, 1))
        sb = lambda n, shape, dt=F32: c.sb(f"{name}_{n}", shape, dt, ctx)
        pad = QTAPS - 1
        pre = sb("preconv", [P, 3, L + pad])
        beta = sb("beta", [P, L])
        qkv = sb("qkv", [P, 3, L])
        sq = sb("squares", [P, 2, L])
        kb = sb("k_beta", [P, L])
        vb = sb("v_beta", [P, L])
        vp = sb("v_padded", [P, L + LONG - 1])
        fl = sb("long_by_channels", [P, 2, L])
        pt = pre[:, 0:2, pad:pad + L]
        fs = sb("short_by_channels", [P, L])
        km = sb("k_by_heads", [P, DH, L])
        nat = sb("k_kb_vb_tokens", [P, TPB, 3, P])
        br = sb("branches", [P, 4, L])
        am = sb("a_upper", [P, 2, DH * P])
        loc = sb("qk_masked", [P, TPB, DH * P])
        xt = sb("inverse_upper", [P, 2, DH * P])
        xc = sb("inverse_compact", [P, 2, P])
        yc = sb("ax_compact", [P, 2, P])
        yb = sb("ax_blocks", [P, 2, DH * P])
        tm = sb("masked", [P, 2, DH * P])
        u = sb("u_tokens", [P, TPB, P])
        wn = sb("w_tokens", [P, TPB, P])
        wT = sb("w_by_channels", [P, L])
        S_ = sb("state", [P, P])
        ks = sb("state_step", [P, P])
        ut = sb("u_of_tile", [P, 2, P])
        scr = fl
        mean = sb("branch_means", [P, 4 * 32])
        st = sb("statistics", [P, TPB, DH, 16])
        stT = sb("statistics_T", [DH * 16, L])
        sm = sb("gate_small", [P, 4, TPB * DH * 4])
        rows = sb("gate_rows", [P, 64])
        half = sb("neghalf", [P, 32])
        h1 = km[:, 0:2, :]
    S = lambda n: c.sem(f"{name}_{n}")
    s_pj, s_pjc, s_bt = S("projected"), S("projection_copied"), S("beta_ready")
    s_v, s_cv, s_act, s_sq, s_ss, s_ri = S("vector_steps"), S("conv_ready"), S("conv_activated"), S("squares_ready"), S("sums_ready"), S("inverse_norms_ready")
    s_ln = S("logarithms_ready")
    s_kq, s_km, s_tr, s_trc = S("qk_ready"), S("k_by_heads_ready"), S("tokens_transposed"), S("tokens_copied")
    s_at, s_am, s_lc, s_lcm, s_x, s_res = S("a_ready"), S("a_masked"), S("qk_products_ready"), S("qk_masked_ready"), S("inverse_step"), S("residual_ready")
    s_y, s_ym, s_z, s_uw, s_uwc, s_wt, s_wtc = S("ax_ready"), S("ax_masked"), S("xax_ready"), S("uw_ready"), S("uw_copied"), S("w_transposed"), S("wT_copied")
    s_p1, s_ut, s_p2, s_kS, s_S, s_o, s_oc, s_od = S("state_products_ready"), S("u_step_ready"), S("state_step_ready"), S("state_step_masked"), S("state_ready"), S("local_ready"), S("outer_copied"), S("delta_ready")
    s_fp, s_fm, s_fd, s_fs, s_ft, s_ftc = S("pool_sums"), S("pool_products_ready"), S("dve_taps"), S("short_ready"), S("filters_transposed"), S("filters_copied")
    s_vp = S("v_padded_ready")
    s_stt, s_stT, s_stTc, s_h, s_hg, s_lg = S("statistics_ready"), S("statistics_transposed"), S("statistics_T_copied"), S("hidden_ready"), S("hidden_activated"), S("logits_ready")
    s_a2, s_a2d = S("gate_inputs"), S("gate_activations")
    s_y2, s_yT, s_yTc, s_out = S("mixed_ready"), S("y_transposed"), S("yT_copied"), S("out_ready")
    s_gr, s_cst = S("gate_rows_steps"), S("constants_ready")
    HB = lambda h: slice(h * P, (h + 1) * P)
    HC_ = lambda h: slice(h * DK, (h + 1) * DK)
    R = lambda i, n: w[:, DW_ROWS + i:DW_ROWS + i + n]
    NLT = NLV + 1
    pairs = [(2 * i, 2 * i + 1) for i in range(TPB // 2)]
    bank = lambda n, k=0, m=512: c.ps[:, n, k:k + m]
    flat = lambda n: c.ps[:, n:n + 2, :].rearrange("p a n -> p (a n)")
    yT = sq[:, 0, :]

    def start(e, b):
        wait(e, s_res, b)
        alone(e, c)

    def tensor(e):
        e.wait_ge(*prev)
        e.wait_ge(s_w, n_w)
        for b in batches(e):
            start(e, b)
            norm.tensor(e, b)
            e.wait_ge(norm.s_xT, 2 * (b + 1))
            for i in range(4):
                if i >= 2:
                    e.wait_ge(s_pjc, 4 * b + i - 1)
                for k in range(2):
                    m = e.matmul(bank(2 + 2 * (i % 2) + k), w[:, i * P:(i + 1) * P], norm.xT[:, k * 512:(k + 1) * 512], start=True, stop=True)
                m.then_inc(s_pj, 1)
            for i in range(2):
                e.wait_ge(s_sq, 2 * b + i + 1)
                for k in range(2):
                    m = e.matmul(bank(6 * i + k), w[:, DW_ONES:DW_ONES + P], sq[:, i, k * 512:(k + 1) * 512], start=True, stop=True)
                m.then_inc(s_ss, 1)
            e.wait_ge(s_kq, 4 * (b + 1))
            e.wait_ge(s_pjc, 4 * (b + 1))
            for t in range(TPB):
                if t >= 4:
                    e.wait_ge(s_trc, TPB * b + t - 3)
                for i, a in enumerate((qkv[:, 1, :], kb[:, :], vb[:, :], qkv[:, 2, :])):
                    m = e.transpose(bank(2 + t % 4, i * P, P), a[:, t * P:(t + 1) * P], c.ident[:, :])
                m.then_inc(s_tr, 1)
            e.wait_ge(s_km, DH * (b + 1))
            e.wait_ge(s_trc, TPB * (b + 1))
            e.wait_ge(s_ri, 2 * (b + 1))
            for j, pair in enumerate(pairs):
                for p, t in enumerate(pair):
                    T = slice(t * P, (t + 1) * P)
                    if j:
                        e.wait_ge(s_x, NLT * (TPB * b + 2 * j - 2) + 2 * NLT)
                        e.wait_ge(s_uwc, TPB * b + 2 * j)
                    for h in range(DH):
                        m = e.matmul(bank(3 * p, h * P, P), km[:, h, T], kb[:, T], start=True, stop=True)
                    m.then_inc(s_at, 1)
                    for h in range(DH):
                        m = e.matmul(bank(3 * p + 1, h * P, P), km[:, h, T], qkv[:, 0, T], start=True, stop=True)
                    m.then_inc(s_lc, 1)
                for l in range(NLT):
                    n = CT * 2 * (j - 1) + 2 * (l - 1)
                    for p, t in enumerate(pair):
                        if l == 0:
                            e.wait_ge(s_am, TPB * b + t + 1)
                            if j:
                                e.wait_ge(s_wtc, TPB * b + 2 * j)
                        else:
                            e.wait_ge(s_x, NLT * (TPB * b + 2 * j) + 2 * (l - 1) + p + 1)
                        for h in range(DH):
                            rhs = mk[:, DM_C:DM_C + CS] if l == 0 else xc[:, p, HC_(h)]
                            m = e.matmul(bank(3 * p + 2, h * CS, CS), am[:, p, HB(h)], rhs, start=True, stop=True)
                        m.then_inc(s_y, 1)
                        if j and l > 1 and p == 0:
                            state_step(e, b, n - 1)
                    if l == 0:
                        continue
                    if j:
                        state_products(e, b, n)
                    for p, t in enumerate(pair):
                        e.wait_ge(s_ym, NLV * (TPB * b + 2 * j) + 2 * (l - 1) + p + 1)
                        if l < NLV:
                            for h in range(DH):
                                e.matmul(bank(3 * p + 2, P + h * CS, CS), xt[:, p, HB(h)], yc[:, p, HC_(h)], start=True, stop=True)
                        for h in range(DH):
                            m = e.matmul(bank(3 * p, h * P, P), yb[:, p, HB(h)], xt[:, p, HB(h)], start=True, stop=True)
                        m.then_inc(s_z, 1)
                        if j and p == 0:
                            state_step(e, b, n)
                    if j:
                        state_products(e, b, n + 1)
                if j:
                    state_step(e, b, CT * 2 * j - 1)
                for p, t in enumerate(pair):
                    e.wait_ge(s_x, NLT * (TPB * b + 2 * j) + 2 * NLV + p + 1)
                    e.wait_ge(s_lcm, TPB * b + t + 1)
                    for h in range(DH):
                        m = e.matmul(bank(3 * p + 1, h * 2 * DK, 2 * DK).rearrange("p (a d) -> p a d", a=2), xt[:, p, HB(h)], nat[:, t, 1:3, HC_(h)], start=True, stop=True)
                    m.then_inc(s_uw, 1)
                for p, t in enumerate(pair):
                    e.wait_ge(s_uwc, TPB * b + t + 1)
                    e.transpose(bank(3 * p + 2, 2 * P, P), wn[:, t, :], c.ident[:, :]).then_inc(s_wt, 1)
            e.wait_ge(s_wtc, TPB * (b + 1))
            for n in range(NCH - 2 * CT, NCH):
                state_products(e, b, n)
                state_step(e, b, n)
            e.wait_ge(s_S, (NCH + 1) * (b + 1))
            local_products(e, b, TPB - 1)
            e.wait_ge(s_fd, LS * (b + 1))
            e.wait_ge(s_fs, SHORT * (b + 1))
            for i, a in enumerate((fs[:, :], fl[:, 0, :])):
                for t in range(TPB):
                    m = e.transpose(bank(2 * i + t // 4, (t % 4) * P, P), a[:, t * P:(t + 1) * P], c.ident[:, :])
                m.then_inc(s_ft, 1)
            e.wait_ge(s_stt, b + 1)
            alone(e, c)
            for t in range(TPB):
                m = e.transpose(c.ps[0:DH * 16, 4 + t // 4, (t % 4) * P:(t % 4 + 1) * P], st[:, t, :, :].rearrange("p h n -> p (h n)"), c.ident[:, :])
            m.then_inc(s_stT, 1)
            e.wait_ge(s_stTc, b + 1)
            for h in range(DH):
                if h >= 2:
                    e.wait_ge(s_hg, DH * b + h - 1)
                for k in range(2):
                    q = slice(k * 512, (k + 1) * 512)
                    e.matmul(bank(2 * (h % 2) + k), w[:, DW_W1:DW_W1 + P], norm.xT[:, q], start=True, stop=False)
                    m = e.matmul(bank(2 * (h % 2) + k), w1s[:, h, :], stT[:, q], start=False, stop=True)
                m.then_inc(s_h, 1)
                if h:
                    logits(e, b, h - 1)
            logits(e, b, DH - 1)
            e.wait_ge(s_y2, b + 1)
            for t in range(TPB):
                m = e.transpose(bank(t // 4, (t % 4) * P, P), br[:, 0, t * P:(t + 1) * P], c.ident[:, :])
            m.then_inc(s_yT, 1)
            e.wait_ge(s_yTc, b + 1)
            for t in range(TPB):
                m = e.matmul(bank(2 + t // 4, (t % 4) * P, P), yT[:, t * P:(t + 1) * P], w[:, DW_O:DW_O + P], start=True, stop=True)
            m.then_inc(s_out, 1)

    def state_products(e, b, n):
        t, r, cols = n // CT, slice((n % CT) * CS, (n % CT + 1) * CS), slice(n * CS, (n + 1) * CS)
        e.wait_ge(s_S, (NCH + 1) * b + n + 1)
        if n % CT == 0 and t:
            e.wait_ge(s_oc, TPB * b + t)
        e.matmul(c.ps[r, 6, 0:P], wT[:, cols], S_[:, :], start=True, stop=True)
        e.matmul(c.ps[r, 6, P:2 * P], qkv[:, 0, cols], S_[:, :], start=True, stop=True).then_inc(s_p1, 1)
        if n % CT == 0 and t:
            local_products(e, b, t - 1)

    def local_products(e, b, t):
        for h in range(DH):
            m = e.matmul(bank(7, P + h * DK, DK), loc[:, t, HB(h)], ut[:, t % 2, HC_(h)], start=True, stop=True)
        m.then_inc(s_o, 1)

    def state_step(e, b, n):
        t, r = n // CT, slice((n % CT) * CS, (n % CT + 1) * CS)
        e.wait_ge(s_ut, NCH * b + n + 1)
        if n % CT == 0 and t:
            e.wait_ge(s_od, TPB * b + t)
        e.matmul(bank(7, 0, P), nat[r, t, 0, :], ut[r, t % 2, :], start=True, stop=True).then_inc(s_p2, 1)

    def logits(e, b, h):
        e.wait_ge(s_hg, DH * b + h + 1)
        for t in range(TPB):
            m = e.matmul(bank(6, (t * DH + h) * 4, 4), h1[:, h % 2, t * P:(t + 1) * P], w[:, DW_W2:DW_W2 + 4], start=True, stop=True)
        m.then_inc(s_lg, 1)

    def outer_copy(e, b, t):
        e.wait_ge(s_ut, NCH * b + CT * (t + 1))
        e.activation(br[:, 2, t * P:(t + 1) * P], bank(6, P, P), ACT.Copy).then_inc(s_oc, 1)

    def scalar(e):
        e.wait_ge(*prev)
        e.wait_ge(s_w, n_w)
        e.wait_ge(s_cst, 4)
        e.activation(rows[:, 0:4], R(20, 4), ACT.Exp).then_inc(s_gr, 1)
        e.wait_ge(s_gr, 1)
        e.activation(rows[:, 0:4], rows[:, 0:4], ACT.Ln, bias=1.0).then_inc(s_gr, 1)
        e.activation(rows[:, 4:8], R(24, 4), ACT.Sigmoid).then_inc(s_gr, 1)
        for b in batches(e):
            start(e, b)
            norm.scalar(e, b)
            for i in range(4):
                e.wait_ge(s_pj, 4 * b + i + 1)
                if i < 3:
                    e.activation(pre[:, i, pad:pad + L], flat(2 + 2 * (i % 2)), ACT.Copy).then_inc(s_pjc, 1)
                else:
                    e.activation(beta[:, :], flat(2 + 2 * (i % 2)), ACT.Sigmoid).then_inc(s_pjc, 1)
            for i in range(3):
                e.wait_ge(s_cv, QTAPS * (3 * b + i + 1))
                e.activation(qkv[:, i, :], km[:, i, :], ACT.Silu).then_inc(s_act, 1)
            e.wait_ge(s_act, 3 * (b + 1))
            e.activation(vp[:, LONG - 1:LONG - 1 + L], qkv[:, 2, :], ACT.Copy).then_inc(s_vp, 1)
            for i in range(2):
                e.activation(sq[:, i, :], qkv[:, i, :], ACT.Square).then_inc(s_sq, 1)
            for i in range(2):
                e.wait_ge(s_ss, 2 * b + i + 1)
                e.activation(sq[:, i, :], flat(6 * i), ACT.Ln, bias=rows[:, 16:17]).then_inc(s_ln, 1)
            for i in range(2):
                e.wait_ge(s_ln, 2 * b + i + 1)
                e.activation(sq[:, i, :], sq[:, i, :], ACT.Exp, scale=-0.5).then_inc(s_ri, 1)
            e.wait_ge(s_kq, 4 * b + 2)
            for h in range(DH):
                e.activation(km[:, h, :], qkv[:, 1, :], ACT.Copy, scale=w[:, DW_HM + h:DW_HM + h + 1]).then_inc(s_km, 1)
            for t in range(TPB):
                e.wait_ge(s_tr, TPB * b + t + 1)
                e.activation(nat[:, t, :, :].rearrange("p a d -> p (a d)"), bank(2 + t % 4, 0, 3 * P), ACT.Copy)
                e.activation(br[:, 3, t * P:(t + 1) * P], bank(2 + t % 4, 3 * P, P), ACT.Copy).then_inc(s_trc, 1)
            for j, pair in enumerate(pairs):
                if j:
                    for t in pairs[j - 1]:
                        outer_copy(e, b, t)
                for p, t in enumerate(pair):
                    e.wait_ge(s_uw, TPB * b + t + 1)
                    src = bank(3 * p + 1, 0, DH * 2 * DK).rearrange("p (h a d) -> p a h d", h=DH, a=2)
                    e.activation(u[:, t, :].rearrange("p (h d) -> p h d", h=DH), src[:, 1], ACT.Copy)
                    e.activation(wn[:, t, :].rearrange("p (h d) -> p h d", h=DH), src[:, 0], ACT.Copy).then_inc(s_uwc, 1)
                for p, t in enumerate(pair):
                    e.wait_ge(s_wt, TPB * b + t + 1)
                    e.activation(wT[:, t * P:(t + 1) * P], bank(3 * p + 2, 2 * P, P), ACT.Copy).then_inc(s_wtc, 1)
            for t in pairs[-1]:
                outer_copy(e, b, t)
            for i in range(2):
                e.wait_ge(s_ft, 2 * b + i + 1)
                e.activation(br[:, i, :], flat(2 * i), ACT.Copy).then_inc(s_ftc, 1)
            for i in range(2):
                e.wait_ge(s_a2, 6 * b + 2 * i + 1)
                e.activation(h1[:, :, :].rearrange("p a n -> p (a n)"), br[:, 2 * i:2 * i + 2, :].rearrange("p a n -> p (a n)"), ACT.Square).then_inc(s_a2d, 1)
                e.wait_ge(s_a2, 6 * b + 2 * i + 2)
                e.activation(scr[:, :, :].rearrange("p a n -> p (a n)"), scr[:, :, :].rearrange("p a n -> p (a n)"), ACT.Square).then_inc(s_a2d, 1)
            e.wait_ge(s_a2, 6 * b + 5)
            e.activation(st[:, :, :, :].rearrange("p t h (k s) -> p (t h k) s", s=4)[:, :, 3], st[:, :, :, :].rearrange("p t h (k s) -> p (t h k) s", s=4)[:, :, 3], ACT.Sqrt).then_inc(s_stt, 1)
            e.wait_ge(s_stT, b + 1)
            e.activation(stT[:, :], c.ps[0:DH * 16, 4:6, :].rearrange("p a n -> p (a n)"), ACT.Copy).then_inc(s_stTc, 1)
            for h in range(DH):
                e.wait_ge(s_h, DH * b + h + 1)
                if h >= 2:
                    e.wait_ge(s_lg, DH * b + h - 1)
                e.activation(h1[:, h % 2, :], flat(2 * (h % 2)), ACT.Gelu, bias=w[:, DW_B1:DW_B1 + 1]).then_inc(s_hg, 1)
            e.wait_ge(s_a2, 6 * b + 6)
            e.activation(sm[:, 1, :], sm[:, 0, :], ACT.Exp).then_inc(s_a2d, 1)
            e.wait_ge(s_v, NV * b + V_MIX)
            e.activation(scr[:, 1, :], br[:, 0, :], ACT.Square).then_inc(s_a2d, 1)
            e.wait_ge(s_yT, b + 1)
            e.activation(yT, flat(0), ACT.Copy).then_inc(s_yTc, 1)

    def u_step(e, b, n):
        t, r = n // CT, slice((n % CT) * CS, (n % CT + 1) * CS)
        if n % CT == 0 and t >= 2:
            e.wait_ge(s_o, TPB * b + t - 1)
        e.wait_ge(s_p1, NCH * b + n + 1)
        e.tensor_tensor(ut[r, t % 2, :], u[r, t, :], c.ps[r, 6, 0:P], ALU.subtract).then_inc(s_ut, 1)
        if n % CT == 0 and t:
            add_local(e, b, t - 1)

    def add_local(e, b, t):
        e.wait_ge(s_o, TPB * b + t + 1)
        e.wait_ge(s_oc, TPB * b + t + 1)
        e.tensor_tensor(br[:, 2, t * P:(t + 1) * P], br[:, 2, t * P:(t + 1) * P], bank(7, P, P), ALU.add).then_inc(s_od, 1)

    def new_state(e, b, n):
        e.wait_ge(s_p2, NCH * b + n + 1)
        e.tensor_tensor(ks[:, :], bank(7, 0, P), mk[:, DM_BD:DM_BD + P], ALU.mult).then_inc(s_kS, 1)
        e.wait_ge(s_kS, NCH * b + n + 1)
        e.wait_ge(s_S, (NCH + 1) * b + n + 1)
        e.tensor_tensor(S_[:, :], S_[:, :], ks[:, :], ALU.add).then_inc(s_S, 1)

    def dve_tap(e, b, n):
        if n < SHORT:
            out, src, tap, k, sem, per = fs[:, :], vp[:, LONG - SHORT + n:LONG - SHORT + n + L], DW_FS + n, n, s_fs, SHORT
        else:
            j = LP + n - SHORT
            out, src, tap, k, sem, per = fl[:, 0, :], vp[:, j:j + L], DW_FL + j, n - SHORT, s_fd, LS
        if k == 0:
            e.tensor_scalar(out, src, w[:, tap:tap + 1], None, ALU.mult).then_inc(sem, 1)
        else:
            e.wait_ge(sem, per * b + k)
            e.scalar_tensor_tensor(out=out, in0=src, scalar=w[:, tap:tap + 1], in1=out, op0=ALU.mult, op1=ALU.add).then_inc(sem, 1)

    def pool_taps(e, b):
        for j in range(LP):
            tap, src = w[:, DW_FL + j:DW_FL + j + 1], vp[:, j:j + L]
            if j >= 2:
                e.wait_ge(s_fp, (LP - 1) * b + j - 1)
                alone(e, c)
            dst = fl[:, 1, :] if j == 0 else pt[:, j % 2, :]
            e.tensor_scalar(dst, src, tap, None, ALU.mult).then_inc(s_fm, 1)
            if j:
                e.wait_ge(s_fm, LP * b + j + 1)
                if j > 1:
                    e.wait_ge(s_fp, (LP - 1) * b + j - 1)
                alone(e, c)
                e.tensor_tensor(fl[:, 1, :], fl[:, 1, :], pt[:, j % 2, :], ALU.add).then_inc(s_fp, 1)

    LP, LD = POOL_TAPS, LONG - POOL_TAPS
    LS = LD + 1
    NV, V_MIX = 35, 33

    def vector(e):
        e.wait_ge(*prev)
        e.wait_ge(s_w, n_w)
        e.memset(pre[:, :, 0:pad], 0.0).then_inc(s_cst, 1)
        e.memset(vp[:, 0:LONG - 1], 0.0).then_inc(s_cst, 1)
        e.memset(rows[:, 16:17], 1e-6).then_inc(s_cst, 1)
        e.memset(ut[:, :, :], 0.0).then_inc(s_cst, 1)
        e.wait_ge(s_cst, 4)
        e.wait_ge(s_gr, 3)
        e.tensor_scalar(rows[:, 0:4], rows[:, 0:4], 1e-4, None, ALU.add).then_inc(s_gr, 1)
        e.wait_ge(s_gr, 4)
        e.reciprocal(rows[:, 8:12], rows[:, 0:4]).then_inc(s_gr, 1)
        e.tensor_scalar(rows[:, 4:8], rows[:, 4:8], 0.5, None, ALU.mult).then_inc(s_gr, 1)
        e.tensor_tensor(rows[:, 20:36].rearrange("p (h n) -> p h n", h=DH), R(4, 16).rearrange("p (h n) -> p h n", h=DH), R(0, 4).unsqueeze(1).to_broadcast([P, DH, 4]), ALU.add).then_inc(s_gr, 1)
        e.wait_ge(s_gr, 7)
        ch = Chain(e, s_v)

        def rest(b):
            start(e, b)
            ch.at(NV * b)

            def step(ins):
                ch(ins)
                ch.sync()

            for i in range(3):
                e.wait_ge(s_pjc, 4 * b + i + 1)
                for j in range(QTAPS):
                    tap = w[:, DW_CV + QTAPS * i + j:DW_CV + QTAPS * i + j + 1]
                    src = pre[:, i, j:j + L]
                    if j == 0:
                        alone(e, c)
                        e.tensor_scalar(km[:, i, :], src, tap, None, ALU.mult).then_inc(s_cv, 1)
                    else:
                        e.wait_ge(s_cv, QTAPS * (3 * b + i) + j)
                        e.scalar_tensor_tensor(out=km[:, i, :], in0=src, scalar=tap, in1=km[:, i, :], op0=ALU.mult, op1=ALU.add).then_inc(s_cv, 1)
            e.wait_ge(s_act, 3 * (b + 1))
            e.wait_ge(s_pjc, 4 * (b + 1))
            e.tensor_tensor(vb[:, :], qkv[:, 2, :], beta[:, :], ALU.mult).then_inc(s_kq, 1)
            for i in (1, 0):
                e.wait_ge(s_ri, 2 * b + 2)
                e.wait_ge(s_sq, 2 * (b + 1))
                e.tensor_tensor(qkv[:, i, :], qkv[:, i, :], sq[:, i, :], ALU.mult).then_inc(s_kq, 1)
                if i == 1:
                    e.wait_ge(s_kq, 4 * b + 2)
                    e.tensor_tensor(kb[:, :], qkv[:, 1, :], beta[:, :], ALU.mult).then_inc(s_kq, 1)
            e.memset(S_[:, :], 0.0).then_inc(s_S, 1)
            e.wait_ge(s_vp, b + 1)
            alone(e, c)
            tap = 0
            for j, pair in enumerate(pairs):
                for p, t in enumerate(pair):
                    e.wait_ge(s_at, TPB * b + t + 1)
                    if j:
                        e.wait_ge(s_uw, TPB * b + 2 * j)
                    e.tensor_tensor(am[:, p, :].rearrange("p (h n) -> p h n", h=DH), bank(3 * p).rearrange("p (h n) -> p h n", h=DH), H4(mk[:, DM_UP:DM_UP + P]), ALU.mult).then_inc(s_am, 1)
                    e.wait_ge(s_lc, TPB * b + t + 1)
                    e.tensor_tensor(loc[:, t, :].rearrange("p (h n) -> p h n", h=DH), bank(3 * p + 1).rearrange("p (h n) -> p h n", h=DH), H4(mk[:, DM_IN:DM_IN + P]), ALU.mult).then_inc(s_lcm, 1)
                for l in range(NLT):
                    cm = mk[:, DM_C + CS * (1 + l):DM_C + CS * (2 + l)].unsqueeze(1).to_broadcast([P, DH, CS])
                    if l == 0:
                        for p, t in enumerate(pair):
                            e.wait_ge(s_am, TPB * b + t + 1)
                            e.tensor_tensor(tm[:, p, :].rearrange("p (h n) -> p h n", h=DH), am[:, p, :].rearrange("p (h n) -> p h n", h=DH), H4(mk[:, DM_M:DM_M + P]), ALU.mult).then_inc(s_t1, 1)
                            e.wait_ge(s_t1, 2 * (TPB * b + t) + 1)
                            e.tensor_tensor(xt[:, p, :].rearrange("p (h n) -> p h n", h=DH), tm[:, p, :].rearrange("p (h n) -> p h n", h=DH), H4(mk[:, DM_ID:DM_ID + P]), ALU.add).then_inc(s_t2, 1)
                            e.wait_ge(s_y, NLT * (TPB * b + 2 * j) + p + 1)
                            e.tensor_tensor(yc[:, p, :].rearrange("p (h n) -> p h n", h=DH), bank(3 * p + 2, 0, P).rearrange("p (h n) -> p h n", h=DH), cm, ALU.mult).then_inc(s_t1, 1)
                            e.wait_ge(s_t1, 2 * (TPB * b + t) + 2)
                            e.wait_ge(s_t2, TPB * b + t + 1)
                            e.tensor_tensor(xc[:, p, :].rearrange("p (h n) -> p h n", h=DH), yc[:, p, :].rearrange("p (h n) -> p h n", h=DH), mk[:, DM_C:DM_C + CS].unsqueeze(1).to_broadcast([P, DH, CS]), ALU.add).then_inc(s_x, 1)
                        continue
                    n = CT * 2 * (j - 1) + 2 * (l - 1)
                    bm = mk[:, DM_M + P * l:DM_M + P * (l + 1)].rearrange("p (r n) -> p r n", r=CT).unsqueeze(1).to_broadcast([P, DH, CT, CS])
                    for p, t in enumerate(pair):
                        e.wait_ge(s_y, NLT * (TPB * b + 2 * j) + 2 * l + p + 1)
                        src = bank(3 * p + 2, 0, P).rearrange("p (h n) -> p h n", h=DH)
                        if l < NLV:
                            e.tensor_tensor(yc[:, p, :].rearrange("p (h n) -> p h n", h=DH), src, cm, ALU.mult)
                        e.tensor_tensor(yb[:, p, :].rearrange("p (h r n) -> p h r n", h=DH, r=CT), src.unsqueeze(2).to_broadcast([P, DH, CT, CS]), bm, ALU.mult).then_inc(s_ym, 1)
                        if j and l > 1 and p == 0:
                            new_state(e, b, n - 1)
                    if j:
                        if l == 1:
                            e.wait_ge(s_wtc, TPB * b + 2 * j)
                        u_step(e, b, n)
                    if l > 1 or j == 0:
                        dve_tap(e, b, tap)
                        tap += 1
                    for p, t in enumerate(pair):
                        e.wait_ge(s_z, NLV * (TPB * b + 2 * j) + 2 * (l - 1) + p + 1)
                        e.wait_ge(s_x, NLT * (TPB * b + 2 * j) + 2 * (l - 1) + p + 1)
                        if l < NLV:
                            e.tensor_tensor(xc[:, p, :], xc[:, p, :], bank(3 * p + 2, P, P), ALU.add)
                        e.tensor_tensor(xt[:, p, :], xt[:, p, :], bank(3 * p), ALU.add).then_inc(s_x, 1)
                        if j and p == 0:
                            new_state(e, b, n)
                    if j:
                        u_step(e, b, n + 1)
                if j:
                    new_state(e, b, CT * 2 * j - 1)
            e.wait_ge(s_wtc, TPB * (b + 1))
            for n in range(NCH - 2 * CT, NCH):
                u_step(e, b, n)
                new_state(e, b, n)
            add_local(e, b, TPB - 1)
            while tap < SHORT + LD:
                dve_tap(e, b, tap)
                tap += 1
            e.wait_ge(s_fp, (LP - 1) * (b + 1))
            e.wait_ge(s_fd, LS * b + LD)
            e.tensor_tensor(fl[:, 0, :], fl[:, 0, :], fl[:, 1, :], ALU.add).then_inc(s_fd, 1)
            e.wait_ge(s_ftc, 2 * (b + 1))
            e.wait_ge(s_od, TPB * (b + 1))
            e.wait_ge(s_trc, TPB * (b + 1))
            G = 2 * TPB * DH

            def slot(i, s):
                v = st[:, :, :, :].rearrange("p t h (k s) -> p t h k s", s=4)[:, :, :, 2 * i:2 * i + 2, s]
                return v.rearrange("p t h k -> p k (t h)")

            flat2 = lambda a: a.rearrange("p a n -> p (a n)")
            grp = lambda a: flat2(a).rearrange("p (g d) -> p g d", d=DK)
            small = lambda a: a.rearrange("p (k g) -> p k g", k=2)
            for i in range(2):
                src = br[:, 2 * i:2 * i + 2, :]
                e.sem_inc(s_a2, 1)
                step(e.tensor_reduce(mean[:, 0:G], grp(src), axis=AXX, op=ALU.add))
                step(e.tensor_scalar(mean[:, 0:G], mean[:, 0:G], 1.0 / DK, None, ALU.mult))
                e.tensor_copy(slot(i, 0), small(mean[:, 0:G]))
                step(e.tensor_tensor(grp(scr[:, :, :]), grp(src), mean[:, 0:G].unsqueeze(2).to_broadcast([P, G, DK]), ALU.subtract))
                e.sem_inc(s_a2, 1)
                step(e.tensor_reduce(mean[:, 0:G], grp(src), axis=AXX, op=ALU.add, apply_absolute_value=True))
                step(e.tensor_scalar(slot(i, 2), small(mean[:, 0:G]), 1.0 / DK, None, ALU.mult))
                e.wait_ge(s_a2d, 6 * b + 2 * i + 1)
                step(e.tensor_reduce(mean[:, G:2 * G], grp(h1[:, :, :]), axis=AXX, op=ALU.add))
                e.tensor_copy(slot(i, 3), small(mean[:, G:2 * G]))
                e.wait_ge(s_a2d, 6 * b + 2 * i + 2)
                step(e.tensor_reduce(mean[:, 0:G], grp(scr[:, :, :]), axis=AXX, op=ALU.add))
                step(e.tensor_scalar(slot(i, 1), small(mean[:, 0:G]), 1.0 / DK, None, ALU.mult))
            e.sem_inc(s_a2, 1)
            V = lambda k: sm[:, k, :].rearrange("p (t n) -> p t n", t=TPB)
            V4 = lambda k: sm[:, k, :].rearrange("p (g n) -> p g n", n=4)
            g1 = mean[:, 0:32]
            g1b = g1.unsqueeze(2).to_broadcast([P, TPB * DH, 4])
            e.wait_ge(s_lg, DH * (b + 1))
            step(e.tensor_tensor(V(0), bank(6, 0, P).rearrange("p (t n) -> p t n", t=TPB), rows[:, 20:36].unsqueeze(1).to_broadcast([P, TPB, 16]), ALU.add))
            tinv = rows[:, 8:12].unsqueeze(2).to_broadcast([P, DH, 4])
            for t in range(TPB):
                m = e.tensor_tensor(sm[:, 2, t * 16:(t + 1) * 16].rearrange("p (h n) -> p h n", h=DH), sm[:, 0, t * 16:(t + 1) * 16].rearrange("p (h n) -> p h n", h=DH), tinv, ALU.mult)
                m.then_inc(s_t3, 1)
            e.wait_ge(s_t3, TPB * (b + 1))
            step(e.tensor_reduce(g1, V4(2), axis=AXX, op=ALU.max))
            e.tensor_tensor(V4(0), V4(2), g1b, ALU.subtract).then_inc(s_a2, 1)
            e.wait_ge(s_a2d, 6 * b + 5)
            step(e.tensor_reduce(g1, V4(1), axis=AXX, op=ALU.add))
            step(e.reciprocal(g1, g1))
            step(e.tensor_tensor(V4(2), V4(1), g1b, ALU.mult))
            e.tensor_scalar(V4(2)[:, :, 0:2], V4(2)[:, :, 0:2], 0.05, None, ALU.max)
            step(e.tensor_scalar(V4(2)[:, :, 2:4], V4(2)[:, :, 2:4], 0.0, None, ALU.max))
            step(e.tensor_reduce(g1, V4(2), axis=AXX, op=ALU.add))
            step(e.reciprocal(g1, g1))
            step(e.tensor_tensor(V4(3), V4(2), g1b, ALU.mult))
            p0 = sm[:, 3, :].rearrange("p (t h n) -> p t h n", t=TPB, n=4)[:, :, :, 0]
            step(e.tensor_tensor(p0, p0, rows[:, 4:8].unsqueeze(1).to_broadcast([P, TPB, DH]), ALU.add))
            g = lambda a: a.rearrange("p (g d) -> p g d", d=DK)
            for k in range(4):
                m = e.tensor_tensor(g(br[:, k, :]), g(br[:, k, :]), V4(3)[:, :, k].unsqueeze(2).to_broadcast([P, TPB * DH, DK]), ALU.mult)
                ch(m)
            ch.sync()
            ch(e.tensor_tensor(br[:, 0, :], br[:, 0, :], br[:, 1, :], ALU.add))
            step(e.tensor_tensor(br[:, 2, :], br[:, 2, :], br[:, 3, :], ALU.add))
            step(e.tensor_tensor(br[:, 0, :], br[:, 0, :], br[:, 2, :], ALU.add))
            mix = ch.n
            e.wait_ge(s_a2d, 6 * b + 6)
            step(e.tensor_reduce(g1, g(scr[:, 1, :]), axis=AXX, op=ALU.add))
            e.tensor_scalar(mean[:, 32:64], g1, 1.0 / DK, 1e-5, ALU.mult, ALU.add).then_inc(s_ms, 1)
            e.wait_ge(s_rr, b + 1)
            step(e.tensor_tensor(g(br[:, 0, :]), g(br[:, 0, :]), mean[:, 64:96].unsqueeze(2).to_broadcast([P, TPB * DH, DK]), ALU.mult))
            e.tensor_tensor(br[:, 0, :].rearrange("p (t d) -> p t d", d=P), br[:, 0, :].rearrange("p (t d) -> p t d", d=P), R(28, P).unsqueeze(1).to_broadcast([P, TPB, P]), ALU.mult).then_inc(s_y2, 1)
            e.wait_ge(s_out, b + 1)
            xb = c.x[:, ds(b * TPB, TPB), :].rearrange("p t d -> p (t d)")
            e.tensor_tensor(xb, xb, flat(2), ALU.add).then_inc(s_res, 1)
            assert (ch.n, mix) == (NV, V_MIX), (ch.n, mix)

        one_ahead(e, lambda b: norm.vector(e, b), rest)

    s_t1, s_t2, s_t3, s_ms, s_rr = S("first_blocks_masked"), S("first_inverse"), S("logits_scaled"), S("mean_squares_ready"), S("rms_inverse_ready")

    def gpsimd(e):
        e.wait_ge(*prev)
        e.wait_ge(s_w, n_w)
        e.memset(half[:, :], -0.5).then_inc(s_hf, 1)
        e.wait_ge(s_hf, 1)

        def rest(b):
            start(e, b)
            e.wait_ge(s_vp, b + 1)
            alone(e, c)
            pool_taps(e, b)
            e.wait_ge(s_ms, b + 1)
            e.tensor_tensor(mean[:, 64:96], mean[:, 32:64], half[:, :], ALU.pow).then_inc(s_rr, 1)

        one_ahead(e, lambda b: norm.gpsimd(e, b), rest)

    s_hf = S("pool_constant_set")
    for n, f in (("gpsimd", gpsimd), ("tensor", tensor), ("scalar", scalar), ("vector", vector)):
        core.add(n, f)
    core.prev = (s_res, B)


def layout_delta(f, r, np):
    m = lambda n: f("L0_attn_b_" + n)
    i = np.arange(P)
    same = lambda n: (i[:, None] // n) == (i[None, :] // n)
    one = np.float32
    w1 = m("W1")
    cols = [m("Wq"), m("Wk"), m("Wv"), np.repeat(m("Wb"), DK, 1), same(DK).astype(one), w1[:D], m("Wo"), m("W2"), m("b1")[:, None]]
    cols += [m("conv_q"), m("conv_k"), m("conv_v"), m("fir_short").reshape(P, -1), m("fir_long").reshape(P, -1)]
    cols += [(i[:, None] // DK == np.arange(DH)[None, :]).astype(one)]
    rows = np.concatenate([m("b2"), m("base_bias").reshape(-1), m("log_temp"), m("conv_residual_logit"), np.tile(m("rms_w"), DH)])
    cols += [np.broadcast_to(rows, (P, rows.size))]
    r["w_delta"] = np.ascontiguousarray(np.concatenate(cols, 1))
    pad = np.zeros((DH * 16, DH, P), one)
    for h in range(DH):
        pad[16 * h:16 * h + 16, h] = w1[D:]
    r["delta_w1s"] = pad
    level = lambda n: same(2 * n) & ((i[:, None] // n) % 2 == 1) & ((i[None, :] // n) % 2 == 0)
    levels = [level(2 ** l) for l in range(NLV + 1)]
    chunk = same(CS)
    full = [(chunk & (i[:, None] < i[None, :])).astype(one), (chunk & (i[:, None] <= i[None, :])).astype(one), np.eye(P, dtype=one), chunk.astype(one)]
    full += [-levels[0].T.astype(one)] + [-x.astype(one) for x in levels[1:]]
    small = lambda x: sum(x[:, CS * k:CS * (k + 1)] for k in range(CT)).astype(one)
    full += [small(np.eye(P, dtype=one))] + [-small(x) for x in levels]
    r["delta_masks"] = np.ascontiguousarray(np.concatenate(full, 1))


SH, SP, SN = 4, 64, 64
SI = SH * SP
TAPS = 7
NC_ = TPB
MW_X, MW_Z, MW_DT = 0, 4 * P, 6 * P
MW_OUT = MW_DT + 8
MW_CONV = MW_OUT + 2 * P
MW_CB = MW_CONV + 4 * TAPS
MW_FD = MW_CB + 4
MW_ROWS = MW_FD + 2 * SH
MW_N = MW_ROWS + 20 + SI


def mamba(core, name):
    c = core
    w = load_weights(core, name, "w_mamba")
    tri = core.sb("triangles", [P, 3, P], F32)
    core.load(name, tri, "triangles")
    s_w, n_w = core.s_w[name], core.n_w[name]
    prev = core.prev
    with ExitStack() as ctx:
        norm = Norm(core, name, ctx, (0, 1))
        sb = lambda n, shape, dt=F32: c.sb(f"{name}_{n}", shape, dt, ctx)
        pre = sb("preconv", [P, 4, L + TAPS - 1])
        act = sb("conv_out", [P, 3, L])
        cs = sb("c_padded", [P, L + 2])
        xnat = sb("x_tokens", [P, NC_, SI])
        bnat = sb("b_tokens", [P, NC_, P])
        zs = sb("z_silu", [P, NC_, SI])
        dt = sb("dt", [P, NC_ * 8])
        dta = sb("dt_abs", [P, NC_ * 8])
        dtl = sb("dt_log", [P, NC_ * 8])
        al = sb("a_log_exp", [P, 8])
        a = sb("decay_rates", [P, NC_ * 8])
        dec = sb("decays", [P, 3, NC_ * 8])
        am = sb("rates_masked", [P, 2, SH, P])
        ex = sb("decay_matrix", [P, 2, SH * P])
        gm = sb("cb_masked", [P, 2, P])
        mm = sb("weights", [P, 2 * NC_, SH, P])
        xw = sb("x_decayed", [P, 2, SI])
        y = sb("y", [P, NC_, SI])
        yt = sb("y_inter", [P, 2, SI])
        st = sb("state", [P, SI])
        dg = sb("diag", [P, NC_ * SH])
        sq = sb("squares", [P, SI])
        ms = sb("mean_squares", [P, NC_])
        ri = sb("rms_inv", [P, NC_])
        yT = sb("yT", [P, 2, L])
    S = lambda n: c.sem(f"{name}_{n}")
    s_pj, s_pjc, s_z, s_zc, s_dtr, s_dta, s_dtl, s_a = S("projected"), S("projection_copied"), S("z_ready"), S("z_activated"), S("dt_projected"), S("dt_abs_ready"), S("dt_log_ready"), S("rates_ready")
    s_al, s_pad, s_cv, s_act, s_tr, s_trc = S("a_log_ready"), S("padding_zeroed"), S("conv_steps"), S("conv_activated"), S("tokens_transposed"), S("tokens_copied")
    s_sum, s_dec, s_am, s_d, s_ex, s_g, s_gm, s_m = S("decay_sums_ready"), S("decays_ready"), S("rates_masked"), S("decay_matrix_ready"), S("decay_exp_ready"), S("cb_ready"), S("cb_masked"), S("weights_ready")
    s_yi, s_yic, s_xw, s_yp, s_ds, s_stt, s_ya, s_dg = S("intra_ready"), S("intra_copied"), S("x_decayed_ready"), S("inter_ready"), S("state_step_ready"), S("state_ready"), S("inter_added"), S("diag_ready")
    s_v, s_ms, s_pe, s_ri, s_yn, s_yT, s_yTc, s_o, s_x = S("vector_steps"), S("squares_summed"), S("eps3_added"), S("rms_inv_ready"), S("y_ready"), S("y_transposed"), S("yT_copied"), S("out_ready"), S("residual_ready")
    s_zw = S("z_weighted")
    NVS = 4 + 1
    order = [(i, d) for i in range(NC_) for d in range(2)]

    def chunk(i, d):
        return i if d == 0 else NC_ - 1 - i

    def bank(n, k=0, m=512):
        return c.ps[:, n, k:k + m]

    def start(e, b):
        wait(e, s_x, b)
        alone(e, c)

    def tensor(e):
        e.wait_ge(*prev)
        e.wait_ge(s_w, n_w)
        for b in batches(e):
            start(e, b)
            norm.tensor(e, b)
            e.wait_ge(norm.s_xT, 2 * (b + 1))
            for i in range(4):
                if i >= 2:
                    e.wait_ge(s_pjc, 4 * b + i - 1)
                for k in range(2):
                    m = e.matmul(bank(2 + 2 * (i % 2) + k), w[:, MW_X + i * P:MW_X + (i + 1) * P], norm.xT[:, k * 512:(k + 1) * 512], start=True, stop=True)
                m.then_inc(s_pj, 1)
            for t in range(NC_):
                m = e.matmul(bank(0, 8 * t, 8), norm.xT[:, t * P:(t + 1) * P], w[:, MW_DT:MW_DT + 8], start=True, stop=True)
            m.then_inc(s_dtr, 1)
            for r in range(2):
                if r:
                    e.wait_ge(s_zc, 2 * b + 1)
                for t in range(4):
                    m = e.matmul(bank(6 + t // 2, (t % 2) * SI, SI), norm.xT[:, (4 * r + t) * P:(4 * r + t + 1) * P], w[:, MW_Z:MW_Z + SI], start=True, stop=True)
                m.then_inc(s_z, 1)
            e.wait_ge(s_a, b + 1)
            for k in range(3):
                m = e.matmul(bank(1, 64 * k, 64), tri[:, k, :], a[:, :], start=True, stop=True)
            m.then_inc(s_sum, 1)
            for n, (i, d) in enumerate(order):
                ch = chunk(i, d)
                lo = SN * d
                e.wait_ge(s_am, 16 * b + n + 1)
                if n < 2:
                    e.wait_ge(s_pjc, 4 * b + 4)
                else:
                    e.wait_ge(s_ex, 16 * b + n - 1)
                e.matmul(bank(2 + n % 2), tri[:, 1 - d, :], am[:, n % 2, :, :].rearrange("p h t -> p (h t)"), start=True, stop=True).then_inc(s_d, 1)
                if n == 0:
                    e.wait_ge(s_act, 4 * (b + 1))
                if n >= 2:
                    e.wait_ge(s_gm, 16 * b + n - 1)
                t0 = ch * P + (0 if d == 0 else 2)
                e.matmul(bank(4 + n % 2, 0, P), act[lo:lo + SN, 2, ch * P:(ch + 1) * P], cs[lo:lo + SN, t0:t0 + P], start=True, stop=True).then_inc(s_g, 1)
            tiles = [(k, t) for t in range(NC_) for k in range(3)]
            for g in range(6):
                if g >= 2:
                    e.wait_ge(s_trc, 6 * b + g - 1)
                else:
                    e.wait_ge(s_zc, 2 * (b + 1))
                for q in range(4):
                    k, t = tiles[4 * g + q]
                    m = e.transpose(bank(6 + g % 2, q * P, P), act[:, k, t * P:(t + 1) * P], c.ident[:, :])
                m.then_inc(s_tr, 1)
            e.wait_ge(s_dta, b + 1)
            for t in range(NC_):
                for k in range(2):
                    m = e.matmul(bank(0, SH * t, SH), act[:, k, t * P:(t + 1) * P], w[:, MW_FD + SH * k:MW_FD + SH * (k + 1)], start=(k == 0), stop=(k == 1))
            m.then_inc(s_dg, 1)
            e.wait_ge(s_trc, 6 * (b + 1))
            e.wait_ge(s_m, 16 * (b + 1))
            for n, (i, d) in enumerate(order):
                if n < NC_:
                    intra_tensor(e, b, n)
                ch = chunk(i, d)
                lo = SN * d
                t0 = ch * P + (0 if d == 0 else 2)
                if i > 0:
                    e.wait_ge(s_stt, 16 * b + n - 1)
                    if n >= 4:
                        e.wait_ge(s_ya, 14 * b + n - 3)
                    e.matmul(bank(4 + n % 2, 0, SI), cs[lo:lo + SN, t0:t0 + P], st[lo:lo + SN, :], start=True, stop=True).then_inc(s_yp, 1)
                e.wait_ge(s_xw, 16 * b + n + 1)
                if n >= 2:
                    e.wait_ge(s_stt, 16 * b + n - 1)
                e.matmul(c.ps[lo:lo + SN, 2 + n % 2, 0:SI], bnat[:, ch, lo:lo + SN], xw[:, n % 2, :], start=True, stop=True).then_inc(s_ds, 1)
            e.wait_ge(s_yn, b + 1)
            for k in range(2):
                for t in range(NC_):
                    m = e.transpose(bank(2 * k + t // 4, (t % 4) * P, P), y[:, t, k * P:(k + 1) * P], c.ident[:, :])
                m.then_inc(s_yT, 1)
            e.wait_ge(s_yTc, 2 * (b + 1))
            for t in range(NC_):
                for k in range(2):
                    m = e.matmul(bank(6 + t // 4, (t % 4) * P, P), yT[:, k, t * P:(t + 1) * P], w[:, MW_OUT + k * P:MW_OUT + (k + 1) * P], start=(k == 0), stop=(k == 1))
            m.then_inc(s_o, 1)

    def intra_tensor(e, b, k):
        ch = chunk(*order[k])
        if k >= 2:
            e.wait_ge(s_yic, NC_ * b + k - 1)
        for h in range(SH):
            for d in range(2):
                i = ch if d == 0 else NC_ - 1 - ch
                m = e.matmul(bank(6 + k % 2, SP * h, SP), mm[:, 2 * i + d, h, :], xnat[:, ch, SP * h:SP * (h + 1)], start=(d == 0), stop=(d == 1))
        m.then_inc(s_yi, 1)

    def flat(n):
        return c.ps[:, n:n + 2, :].rearrange("p a n -> p (a n)")

    def scalar(e):
        e.wait_ge(*prev)
        e.wait_ge(s_w, n_w)
        e.activation(al[:, :], w[:, MW_ROWS + 8:MW_ROWS + 16], ACT.Exp).then_inc(s_al, 1)
        for b in batches(e):
            start(e, b)
            norm.scalar(e, b)
            for i in range(4):
                e.wait_ge(s_pj, 4 * b + i + 1)
                e.activation(pre[:, i, 3:3 + L], flat(2 + 2 * (i % 2)), ACT.Copy).then_inc(s_pjc, 1)
            for r in range(2):
                e.wait_ge(s_z, 2 * b + r + 1)
                e.activation(zs[:, 4 * r:4 * r + 4, :].rearrange("p t n -> p (t n)"), flat(6), ACT.Silu).then_inc(s_zc, 1)
            e.wait_ge(s_dta, b + 1)
            e.activation(dtl[:, :], dta[:, :], ACT.Exp, scale=-1.0).then_inc(s_dtl, 1)
            e.wait_ge(s_dtl, 2 * b + 1)
            e.activation(dtl[:, :], dtl[:, :], ACT.Ln, bias=1.0).then_inc(s_dtl, 1)
            e.wait_ge(s_sum, b + 1)
            e.activation(dec[:, :, :].rearrange("p k n -> p (k n)"), bank(1, 0, 192), ACT.Exp).then_inc(s_dec, 1)
            for n in range(16):
                e.wait_ge(s_d, 16 * b + n + 1)
                if n >= 2:
                    e.wait_ge(s_m, 16 * b + n - 1)
                e.activation(ex[:, n % 2, :], bank(2 + n % 2), ACT.Exp).then_inc(s_ex, 1)
                if n == 0:
                    for q, i in enumerate((3, 2, 0, 1)):
                        e.wait_ge(s_cv, TAPS * (4 * b + q + 1))
                        alone(e, c)
                        dst = cs[:, 1:1 + L] if i == 3 else act[:, i, :]
                        e.activation(dst, conv_out[:, i, :], ACT.Silu).then_inc(s_act, 1)
            for g in range(6):
                e.wait_ge(s_tr, 6 * b + g + 1)
                for q in range(4):
                    k, t = (4 * g + q) % 3, (4 * g + q) // 3
                    dst = xnat[:, t, k * P:(k + 1) * P] if k < 2 else bnat[:, t, :]
                    m = e.activation(dst, bank(6 + g % 2, q * P, P), ACT.Copy)
                m.then_inc(s_trc, 1)
            for k in range(NC_):
                e.wait_ge(s_yi, NC_ * b + k + 1)
                e.activation(y[:, chunk(*order[k]), :], bank(6 + k % 2, 0, SI), ACT.Copy).then_inc(s_yic, 1)
            for t in range(NC_):
                e.wait_ge(s_ya, 14 * (b + 1))
                e.wait_ge(s_v, NVS * b + 4)
                if t:
                    e.wait_ge(s_ms, NC_ * b + t)
                e.activation(sq[:, :], y[:, t, :], ACT.Square, accum_out=ms[:, t:t + 1]).then_inc(s_ms, 1)
            for k in range(2):
                e.wait_ge(s_yT, 2 * b + k + 1)
                e.activation(yT[:, k, :], flat(2 * k), ACT.Copy).then_inc(s_yTc, 1)

    conv_out = mm[:, 0:8, :, :].rearrange("p (i a) h t -> p i (a h t)", i=4)

    def vector(e):
        e.wait_ge(*prev)
        e.wait_ge(s_w, n_w)
        e.memset(pre[:, :, 0:3], 0.0).then_inc(s_pad, 1)
        e.memset(pre[:, :, L + 3:L + 6], 0.0).then_inc(s_pad, 1)
        e.memset(cs[:, 0:1], 0.0).then_inc(s_pad, 1)
        e.memset(cs[:, L + 1:L + 2], 0.0).then_inc(s_pad, 1)
        e.wait_ge(s_pad, 4)
        e.wait_ge(s_al, 1)
        ch_ = Chain(e, s_v)

        def rest(b):
            start(e, b)
            ch_.at(NVS * b)

            def step(ins):
                ch_(ins)
                ch_.sync()

            e.wait_ge(s_dtr, b + 1)
            bias = w[:, MW_ROWS:MW_ROWS + 8].unsqueeze(1).to_broadcast([P, NC_, 8])
            step(e.tensor_tensor(dt[:, :].rearrange("p (t n) -> p t n", n=8), bank(0, 0, 64).rearrange("p (t n) -> p t n", n=8), bias, ALU.add))
            e.scalar_tensor_tensor(out=dta[:, :], in0=dt[:, :], scalar=-1.0, in1=dt[:, :], op0=ALU.mult, op1=ALU.max).then_inc(s_dta, 1)
            e.wait_ge(s_dtl, 2 * (b + 1))
            step(e.scalar_tensor_tensor(out=dt[:, :], in0=dt[:, :], scalar=0.0, in1=dtl[:, :], op0=ALU.max, op1=ALU.add))
            alb = al[:, :].unsqueeze(1).to_broadcast([P, NC_, 8])
            e.scalar_tensor_tensor(out=a[:, :].rearrange("p (t n) -> p t n", n=8), in0=dt[:, :].rearrange("p (t n) -> p t n", n=8), scalar=-1.0, in1=alb, op0=ALU.mult, op1=ALU.mult).then_inc(s_a, 1)
            for q, i in enumerate((3, 2, 0, 1)):
                e.wait_ge(s_pjc, 4 * b + i + 1)
                for j in range(TAPS):
                    tap = w[:, MW_CONV + TAPS * i + j:MW_CONV + TAPS * i + j + 1]
                    src = pre[:, i, j:j + L]
                    if j == 0:
                        alone(e, c)
                        e.tensor_scalar(conv_out[:, i, :], src, tap, w[:, MW_CB + i:MW_CB + i + 1], ALU.mult, ALU.add).then_inc(s_cv, 1)
                    else:
                        e.wait_ge(s_cv, TAPS * (4 * b + q) + j)
                        e.scalar_tensor_tensor(out=conv_out[:, i, :], in0=src, scalar=tap, in1=conv_out[:, i, :], op0=ALU.mult, op1=ALU.add).then_inc(s_cv, 1)
            e.wait_ge(s_act, 4 * (b + 1))
            for n, (i, d) in enumerate(order):
                e.wait_ge(s_g, 16 * b + n + 1)
                if n >= 2:
                    e.wait_ge(s_m, 16 * b + n - 1)
                e.tensor_tensor(gm[:, n % 2, :], bank(4 + n % 2, 0, P), tri[:, d, :], ALU.mult).then_inc(s_gm, 1)
                e.wait_ge(s_gm, 16 * b + n + 1)
                e.wait_ge(s_ex, 16 * b + n + 1)
                e.tensor_tensor(mm[:, n, :, :], ex[:, n % 2, :].rearrange("p (h t) -> p h t", h=SH), gm[:, n % 2, :].unsqueeze(1).to_broadcast([P, SH, P]), ALU.mult).then_inc(s_m, 1)
            e.wait_ge(s_dg, b + 1)
            dpb = w[:, MW_ROWS + 16:MW_ROWS + 20].unsqueeze(1).to_broadcast([P, NC_, SH])
            step(e.tensor_tensor(dg[:, :].rearrange("p (t h) -> p t h", h=SH), bank(0, 0, 32).rearrange("p (t h) -> p t h", h=SH), dpb, ALU.add))
            nya = 0
            for n, (i, d) in enumerate(order):
                ch = chunk(i, d)
                lo = SN * d
                if i > 0:
                    db = dec[:, d, 8 * ch + 4 * d:8 * ch + 4 * d + 4].unsqueeze(2).to_broadcast([P, SH, SP])
                    e.wait_ge(s_yp, 14 * b + nya + 1)
                    e.wait_ge(s_ya, 14 * b + nya) if nya else None
                    e.tensor_tensor(yt[:, n % 2, :].rearrange("p (h q) -> p h q", h=SH), bank(4 + n % 2, 0, SI).rearrange("p (h q) -> p h q", h=SH), db, ALU.mult).then_inc(s_yt, 1)
                    e.wait_ge(s_yt, 14 * b + nya + 1)
                    if n < NC_ + 2:
                        e.wait_ge(s_yic, NC_ * b + min(n + 1, NC_))
                    e.tensor_tensor(y[:, ch, :], y[:, ch, :], yt[:, n % 2, :], ALU.add).then_inc(s_ya, 1)
                    nya += 1
                e.wait_ge(s_ds, 16 * b + n + 1)
                if i == 0:
                    e.tensor_copy(st[lo:lo + SN, :], c.ps[lo:lo + SN, 2 + n % 2, 0:SI]).then_inc(s_stt, 1)
                else:
                    tot = dec[lo:lo + SN, 2, 8 * ch + 4 * d:8 * ch + 4 * d + 4].unsqueeze(2).to_broadcast([SN, SH, SP])
                    stv = st[lo:lo + SN, :].rearrange("p (h q) -> p h q", h=SH)
                    e.wait_ge(s_stt, 16 * b + n - 1)
                    e.tensor_tensor(stv, stv, tot, ALU.mult).then_inc(s_stm, 1)
                    e.wait_ge(s_stm, 14 * b + nya)
                    e.tensor_tensor(st[lo:lo + SN, :], st[lo:lo + SN, :], c.ps[lo:lo + SN, 2 + n % 2, 0:SI], ALU.add).then_inc(s_stt, 1)
            e.wait_ge(s_ya, 14 * (b + 1))
            e.wait_ge(s_xd, b + 1)
            step(e.tensor_tensor(y[:, :, :], y[:, :, :], xnat[:, :, :], ALU.add))
            e.wait_ge(s_ri, b + 1)
            e.wait_ge(s_zw, b + 1)
            step(e.tensor_tensor(y[:, :, :], y[:, :, :], ri[:, :].unsqueeze(2).to_broadcast([P, NC_, SI]), ALU.mult))
            e.tensor_tensor(y[:, :, :], y[:, :, :], zs[:, :, :], ALU.mult).then_inc(s_yn, 1)
            e.wait_ge(s_o, b + 1)
            xb = c.x[:, ds(b * TPB, TPB), :].rearrange("p t d -> p (t d)")
            e.tensor_tensor(xb, xb, flat(6), ALU.add).then_inc(s_x, 1)
            assert ch_.n == NVS, ch_.n

        one_ahead(e, lambda b: norm.vector(e, b), rest)

    s_yt, s_stm, s_xd = S("inter_scaled"), S("state_decayed"), S("x_times_diag")

    def gpsimd(e):
        e.wait_ge(*prev)
        e.wait_ge(s_w, n_w)

        def rest(b):
            start(e, b)
            e.wait_ge(s_a, b + 1)
            for n, (i, d) in enumerate(order):
                ch = chunk(i, d)
                if n >= 2:
                    e.wait_ge(s_d, 16 * b + n - 1)
                e.tensor_tensor(am[:, n % 2, :, :], tri[:, d, :].unsqueeze(1).to_broadcast([P, SH, P]),
                                a[:, 8 * ch + 4 * d:8 * ch + 4 * d + 4].unsqueeze(2).to_broadcast([P, SH, P]), ALU.mult).then_inc(s_am, 1)
            e.wait_ge(s_trc, 6 * (b + 1))
            e.wait_ge(s_dec, b + 1)
            for n, (i, d) in enumerate(order):
                ch = chunk(i, d)
                if n >= 2:
                    e.wait_ge(s_ds, 16 * b + n - 1)
                e.tensor_tensor(xw[:, n % 2, :].rearrange("p (h q) -> p h q", h=SH), xnat[:, ch, :].rearrange("p (h q) -> p h q", h=SH),
                                dec[:, 1 - d, 8 * ch + 4 * d:8 * ch + 4 * d + 4].unsqueeze(2).to_broadcast([P, SH, SP]), ALU.mult).then_inc(s_xw, 1)
            e.wait_ge(s_zc, 2 * (b + 1))
            e.tensor_tensor(zs[:, :, :], zs[:, :, :], w[:, MW_ROWS + 20:MW_ROWS + 20 + SI].unsqueeze(1).to_broadcast([P, NC_, SI]), ALU.mult).then_inc(s_zw, 1)
            e.wait_ge(s_v, NVS * b + 3)
            e.wait_ge(s_yi, NC_ * (b + 1))
            e.wait_ge(s_xw, 16 * (b + 1))
            e.tensor_tensor(xnat[:, :, :].rearrange("p t (h q) -> p (t h) q", h=SH), xnat[:, :, :].rearrange("p t (h q) -> p (t h) q", h=SH),
                            dg[:, :].unsqueeze(2).to_broadcast([P, NC_ * SH, SP]), ALU.mult).then_inc(s_xd, 1)
            e.wait_ge(s_ms, NC_ * (b + 1))
            alone(e, c)
            e.tensor_scalar(ri[:, :], ms[:, :], 1.0 / SI, 1e-5, ALU.mult, ALU.add).then_inc(s_pe, 1)
            e.wait_ge(s_pe, b + 1)
            e.tensor_tensor(ri[:, :], ri[:, :], c.neghalf[:, :], ALU.pow).then_inc(s_ri, 1)

        one_ahead(e, lambda b: norm.gpsimd(e, b), rest)

    for n, f in (("gpsimd", gpsimd), ("tensor", tensor), ("scalar", scalar), ("vector", vector)):
        core.add(n, f)
    core.prev = (s_x, B)


def layout_mamba(f, r, np):
    m = lambda n: f("L1_attn_a_" + n)
    wi = m("W_in")
    z, x, bc, dtw = wi[0:256], wi[256:512], wi[512:768], wi[768:776]

    conv, cb = m("conv_w")[:, 0, :], m("conv_b")[:, None]

    def tiles(v, q):
        return [v[0:128], v[128:256], np.concatenate([q[0:64], q[128:192]]), np.concatenate([q[64:128], q[192:256]])]

    cols = [a.T for a in tiles(x, bc)] + [z.T, dtw.T]
    wo = m("W_out").T
    cols += [wo[0:128], wo[128:256]]
    cols += tiles(conv[0:256], conv[256:512]) + tiles(cb[0:256], cb[256:512])
    fd = m("fc_D_w").T
    cols += [fd[0:128], fd[128:256]]
    rows = np.concatenate([m("dt_bias"), m("dt_bias"), m("A_log"), m("A_log"), m("Dp"), m("norm_w")])
    cols += [np.broadcast_to(rows, (P, rows.size))]
    r["w_mamba"] = np.ascontiguousarray(np.concatenate(cols, 1))
    i = np.arange(P)
    r["triangles"] = np.ascontiguousarray(np.stack([i[:, None] < i[None, :], i[:, None] > i[None, :], np.ones((P, P), bool)], 1).astype(np.float32))


NE, NF = 4, 4
VB, OB, G1, B1, G2, B2, RW = range(7)


def moe(core, name, o, o_ready, octx, w, w1, w2, rows):
    c = core
    wo = w[:, 3 * P:4 * P]
    b1 = w[:, 4 * P + 2:4 * P + 2 + NE * NF]
    rb = w[:, 4 * P + 18:4 * P + 19]
    with ExitStack() as ctx:
        norm = Norm(core, name + "_post", ctx, (0, 1))
        on = c.sb(name + "_o_batch", [P, QT, NG, GH * HD], F32, ctx)
        oT = c.sb(name + "_oT", [P, L], F32, ctx)
        x1 = c.sb(name + "_x1", [P, TPB, D], F32, ctx)
        x1T = c.sb(name + "_x1T", [P, L], F32, ctx)
        hid = c.sb(name + "_hidden", [P, 2, NF, L], F32, ctx)
        ff = c.sb(name + "_ff", [P, TPB, D], F32, ctx)
        weighed = c.sb(name + "_router_products", [P, TPB, D], F32, ctx)
        st = c.sb(name + "_stats2", [P, TPB, 6], F32, ctx)
        mv = c.sb(name + "_mv2", [P, TPB, 2], F32, ctx)
        rs = c.sb(name + "_rstd2", [P, TPB], F32, ctx)
        key = c.sb(name + "_key", [P, TPB], F32, ctx)
        kr = c.sb(name + "_key_rounded", [P, TPB], F32, ctx)
        ki = c.sb(name + "_key_int", [P, TPB], I32, ctx)
        kg = c.sb(name + "_key_above", [P, TPB], F32, ctx)
        kq = c.sb(name + "_key_quarter", [P, TPB], F32, ctx)
        mask = c.sb(name + "_mask", [P, NE, TPB], F32, ctx)
    octx.close()
    S = lambda n: c.sem(f"{name}_{n}")
    s_on, s_tp, s_oT, s_y = S("o_staged"), S("oT_transposed"), S("oT_ready"), S("projected_out")
    s_dv, s_var, s_rs, s_epsd = S("vector_steps"), S("variances_ready"), S("rstd2_ready"), S("eps2_added")
    s_x1, s_x1t, s_x1T = S("x1_ready"), S("x1_transposed"), S("x1T_ready")
    s_h, s_hr, s_e, s_ea, s_x = S("hidden_ready"), S("hidden_activated"), S("expert_out_ready"), S("expert_out_added"), S("residual_ready")
    DV = 118

    def gpsimd(e):
        e.wait_ge(*o_ready)
        for b in batches(e):
            norm.gpsimd(e, b)
            wait(e, s_tp, b)
            alone(e, c)
            e.tensor_copy(on[:, :, :, :].rearrange("p t g d -> p g t d"), o[:, ds(b * NG, NG), :, :]).then_inc(s_on, 1)
            for k in range(2):
                e.wait_ge(s_var, 2 * b + k + 1)
                alone(e, c)
                e.tensor_scalar(rs[:, :], mv[:, :, 1], 1e-5, None, ALU.add).then_inc(s_epsd, 1)
                e.wait_ge(s_epsd, 2 * b + k + 1)
                e.tensor_tensor(rs[:, :], rs[:, :], c.neghalf[:, :], ALU.pow).then_inc(s_rs, 1)

    def tensor(e):
        e.wait_ge(*o_ready)
        for b in batches(e):
            e.wait_ge(s_on, b + 1)
            wait(e, s_oT, 2 * b)
            wait(e, s_x1T, 2 * b)
            for t in range(QT):
                m = e.transpose(c.ps[:, t // 4, (t % 4) * P:(t % 4 + 1) * P], on[:, t, :, :].rearrange("p g d -> p (g d)"), c.ident[:, :])
            m.then_inc(s_tp, 1)
            e.wait_ge(s_oT, 2 * (b + 1))
            wait(e, s_ea, NE * b)
            for t in range(QT):
                m = e.matmul(c.ps[:, 2 + t // 4, (t % 4) * P:(t % 4 + 1) * P], oT[:, t * P:(t + 1) * P], wo, start=True, stop=True)
            m.then_inc(s_y, 1)
            e.wait_ge(s_x1, b + 1)
            for t in range(TPB):
                m = e.transpose(c.ps[:, t // 4, (t % 4) * P:(t % 4 + 1) * P], x1[:, t, :], c.ident[:, :])
            m.then_inc(s_x1t, 1)
            e.wait_ge(s_x1T, 2 * (b + 1))
            for x in range(NE + 1):
                if x < NE:
                    for j in range(NF):
                        u = NF * x + j
                        wait(e, s_hr, NE * NF * b + u - 1)
                        for k in range(2):
                            m = e.matmul(c.ps[:, 4 + 2 * (u % 2) + k, :], w1[:, x, j * P:(j + 1) * P], x1T[:, k * 512:(k + 1) * 512], start=True, stop=True)
                        m.then_inc(s_h, 1)
                if x > 0:
                    y = x - 1
                    e.wait_ge(s_hr, NE * NF * b + NF * x)
                    wait(e, s_ea, NE * b + y)
                    for t in range(TPB):
                        for j in range(NF):
                            m = e.matmul(c.ps[:, 2 * (y % 2) + t // 4, (t % 4) * P:(t % 4 + 1) * P], hid[:, y % 2, j, t * P:(t + 1) * P], w2[:, y, j, :],
                                         start=(j == 0), stop=(j == NF - 1))
                    m.then_inc(s_e, 1)

    def scalar(e):
        e.wait_ge(*o_ready)
        for b in batches(e):
            e.wait_ge(s_tp, b + 1)
            wait(e, s_y, b)
            alone(e, c)
            for k in range(2):
                e.activation(oT[:, k * 512:(k + 1) * 512], c.ps[:, k, :], ACT.Copy).then_inc(s_oT, 1)
            e.wait_ge(s_x1t, b + 1)
            wait(e, s_e, NE * b)
            alone(e, c)
            for k in range(2):
                e.activation(x1T[:, k * 512:(k + 1) * 512], c.ps[:, k, :], ACT.Copy).then_inc(s_x1T, 1)
            for x in range(NE):
                for j in range(NF):
                    u = NF * x + j
                    e.wait_ge(s_h, NE * NF * b + u + 1)
                    if j == 0:
                        wait(e, s_e, NE * b + x - 1)
                        alone(e, c)
                    bank = 4 + 2 * (u % 2)
                    e.activation(hid[:, x % 2, j, :], c.ps[:, bank:bank + 2, :].rearrange("p a n -> p (a n)"), ACT.Relu, bias=b1[:, u:u + 1]).then_inc(s_hr, 1)

    def tiled(row):
        return rows[:, row:row + 1, :].to_broadcast([P, TPB, D])

    def vector(e):
        e.wait_ge(*o_ready)
        chain = Chain(e, s_dv)
        for b in batches(e):
            chain.at(DV * b)

            def step(ins):
                chain(ins)
                chain.sync()

            def layer_norm(src, k):
                for t in range(TPB):
                    chain(e.bn_stats(st[:, t, :], src[:, t, :]))
                chain.sync()
                alone(e, c)
                for t in range(TPB):
                    m = e.bn_aggr(mv[:, t, :], st[:, t, :])
                m.then_inc(s_var, 1)
                e.wait_ge(s_var, 2 * b + k + 1)
                e.wait_ge(s_rs, 2 * b + k + 1)
                for t in range(TPB):
                    chain(e.tensor_scalar(src[:, t, :], src[:, t, :], mv[:, t, 0:1], rs[:, t:t + 1], ALU.subtract, ALU.mult))
                chain.sync()

            norm.vector(e, b, transposed=False)
            e.wait_ge(s_y, b + 1)
            e.wait_ge(norm.s_xn, TPB * (b + 1))
            wait(e, s_x1t, b)
            step(e.tensor_tensor(x1[:, :, :].rearrange("p t d -> p (t d)"), norm.xn[:, :, :].rearrange("p t d -> p (t d)"), c.ps[:, 2:4, :].rearrange("p a n -> p (a n)"), ALU.add))
            step(e.tensor_tensor(x1[:, :, :], x1[:, :, :], tiled(OB), ALU.add))
            layer_norm(x1, 0)
            step(e.tensor_tensor(x1[:, :, :], x1[:, :, :], tiled(G1), ALU.mult))
            e.tensor_tensor(x1[:, :, :], x1[:, :, :], tiled(B1), ALU.add).then_inc(s_x1, 1)
            e.wait_ge(s_x1, b + 1)
            step(e.tensor_tensor(weighed[:, :, :], x1[:, :, :], tiled(RW), ALU.mult))
            step(e.tensor_reduce(key[:, :], weighed[:, :, :], AXX, ALU.add))
            step(e.tensor_scalar(key[:, :], key[:, :], rb, None, ALU.add))

            def floor(dst, src):
                step(e.tensor_copy(ki[:, :], src))
                step(e.tensor_copy(kr[:, :], ki[:, :]))
                step(e.tensor_tensor(kg[:, :], kr[:, :], src, ALU.is_gt))
                step(e.tensor_tensor(dst, kr[:, :], kg[:, :], ALU.subtract))

            floor(key[:, :], key[:, :])
            step(e.tensor_scalar(kq[:, :], key[:, :], 0.25, None, ALU.mult))
            floor(kq[:, :], kq[:, :])
            step(e.scalar_tensor_tensor(out=key[:, :], in0=kq[:, :], scalar=-4.0, in1=key[:, :], op0=ALU.mult, op1=ALU.add))
            for x in range(NE):
                chain(e.tensor_scalar(mask[:, x, :], key[:, :], float(x), None, ALU.is_equal))
            chain.sync()
            for x in range(NE):
                for t in range(TPB):
                    src = x1 if x == 0 else ff
                    chain(e.scalar_tensor_tensor(out=ff[:, t, :], in0=rows[:, 7 + x, :], scalar=mask[:, x, t:t + 1], in1=src[:, t, :], op0=ALU.mult, op1=ALU.add))
                chain.sync()
            for x in range(NE):
                e.wait_ge(s_e, NE * b + x + 1)
                for t in range(TPB):
                    src = c.ps[:, 2 * (x % 2) + t // 4, (t % 4) * P:(t % 4 + 1) * P]
                    m = chain(e.scalar_tensor_tensor(out=ff[:, t, :], in0=src, scalar=mask[:, x, t:t + 1], in1=ff[:, t, :], op0=ALU.mult, op1=ALU.add))
                chain.sync()
                alone(e, c)
                e.sem_inc(s_ea, 1)
            layer_norm(ff, 1)
            step(e.tensor_tensor(ff[:, :, :], ff[:, :, :], tiled(G2), ALU.mult))
            step(e.tensor_tensor(ff[:, :, :], ff[:, :, :], tiled(B2), ALU.add))
            xb = c.x[:, ds(b * TPB, TPB), :].rearrange("p t d -> p (t d)")
            e.tensor_tensor(xb, xb, ff[:, :, :].rearrange("p t d -> p (t d)"), ALU.add).then_inc(s_x, 1)
            assert chain.n == DV, chain.n
            e.wait_ge(s_x, b + 1)

    for n, f in (("gpsimd", gpsimd), ("tensor", tensor), ("scalar", scalar), ("vector", vector)):
        core.add(n, f)
    core.prev = (s_x, B)


def layout_moe(f, r, np):
    m = lambda n: f("L1_ffn_" + n)
    col = lambda a: a.reshape(-1, 1)
    b1 = m("b1").reshape(NE * NF, P).T
    r["w_moe"] = np.concatenate([m("Wq"), m("Wk"), m("Wv"), m("Wo"), col(m("bq")), col(m("bk")), b1, np.broadcast_to(m("router_b"), (P, 1))], 1)
    r["moe_w1"] = np.ascontiguousarray(m("W1").transpose(1, 0, 2))
    r["moe_w2"] = np.ascontiguousarray(m("W2").reshape(NE, NF, P, D).transpose(2, 0, 1, 3))
    rows = [m("bv"), m("bo"), m("ln1_g"), m("ln1_b"), m("ln2_g"), m("ln2_b"), m("router_w")[:, 0]] + list(m("b2"))
    r["moe_rows"] = np.ascontiguousarray(np.broadcast_to(np.stack(rows)[None], (P, len(rows), D)))

LAYER_BUILDERS = {'alibi': attn_alibi, 'rmsattn': attn_rms, 'moeattn': attn_moe, 'delta': delta, 'mamba': mamba, 'moe': moe}
LAYOUTS = (layout_attn, layout_delta, layout_mamba, layout_moe, )


LAYERS = ("alibi", "ffn0", "delta", "ffn1", "mamba", "moeattn0", "rmsattn", "moeattn1")


def program(nc, ins, out):
    import numpy as np
    with ExitStack() as ctx:
        core = Core(nc, ctx, ins)
        s_x = core.kept_sem("x_loaded")
        s_const = core.kept_sem("constants_loaded")
        s_set = core.s_set
        s_wi = core.kept_sem("integer_weights_loaded")
        s_wf = core.kept_sem("integer_weights_converted")
        wint = core.sb("wint", [P, 9 * P], I32)
        wffn = core.sb("wffn", [P, 9 * P], F32)
        wg, wu, wd = wffn[:, 0:3 * P], wffn[:, 3 * P:6 * P], wffn[:, 6 * P:9 * P].rearrange("p (j d) -> p j d", j=3)

        def sync_start(e):
            e.dma_start(core.x[:, :, :], ins["x"]).then_inc(s_x, 16)
            e.dma_start(core.ident[:, :], ins["ident"]).then_inc(s_const, 16)
            e.dma_start(wint[:, :], ins["w_int"]).then_inc(s_wi, 16)

        def vector_start(e):
            e.wait_ge(s_const, 16)
            e.tensor_copy(core.ident_bf[:, :], core.ident[:, :]).then_inc(s_set, 1)
            e.memset(core.neghalf[:, :], -0.5).then_inc(s_set, 1)
            e.wait_ge(s_wi, 16)
            e.tensor_copy(wffn[:, :], wint[:, :]).then_inc(s_wf, 1)
            e.wait_ge(s_set, 2)
            e.wait_ge(s_x, 16)

        def other_start(e):
            e.wait_ge(s_set, 2)
            e.wait_ge(s_x, 16)

        core.add("sync", sync_start)
        core.add("vector", vector_start)
        for n in ("tensor", "scalar", "gpsimd"):
            core.add(n, other_start)
        core.prev = (s_x, 16)
        for layer in LAYERS:
            core.begin_layer()
            if layer.startswith("ffn"):
                ffn(core, layer, wg, wu, wd, 1.0 / 127.0, s_wf, 1)
            else:
                LAYER_BUILDERS[layer.rstrip("0123456789")](core, layer)
            core.end_layer()
        prev = core.prev
        s_out = core.kept_sem("output_written")

        def sync_end(e):
            e.wait_ge(*prev)
            e.dma_start(out.rearrange("b (t p) d -> p (b t) d", p=P), core.x[:, :, :]).then_inc(s_out, 16)
            e.wait_ge(s_out, 16)

        core.add("sync", sync_end)
        block = ctx.enter_context(nc.Block())

        @block.sync
        def _(e):
            for part in core.programs["sync"]:
                part(e)

        @block.gpsimd
        def _(e):
            for part in core.programs["gpsimd"]:
                part(e)

        @block.scalar
        def _(e):
            for part in core.programs["scalar"]:
                part(e)

        @block.vector
        def _(e):
            for part in core.programs["vector"]:
                part(e)

        @block.tensor
        def _(e):
            for part in core.programs["tensor"]:
                part(e)


def layout(v):
    import numpy as np
    f = lambda n: np.asarray(v[n])
    r = {}
    r["x"] = np.ascontiguousarray(f("L0_attn_a_x").reshape(NT, P, D).transpose(1, 0, 2))
    r["ident"] = np.eye(P, dtype=np.float32)
    down = f("L0_ffn_w_down").T.reshape(3, P, P).transpose(1, 0, 2).reshape(P, 3 * P)
    r["w_int"] = np.ascontiguousarray(np.concatenate([f("L0_ffn_w_gate").T, f("L0_ffn_w_up").T, down], 1))
    for more in LAYOUTS:
        more(f, r, np)
    return r


def kernel(**inputs):
    import concourse.bacc as bacc
    from concourse.bass_utils import run_bass_kernel_spmd
    import numpy as np
    nc = bacc.Bacc("TRN2", target_bir_lowering=False, num_devices=1)
    arrays = layout(inputs)
    feed, ins = {}, {}
    for name, a in arrays.items():
        feed["in_" + name] = a
        ins[name] = nc.dram_tensor("in_" + name, a.shape, mybir.dt.from_np(a.dtype), kind="ExternalInput").ap()
    out = nc.dram_tensor("out", (B, L, D), F32, kind="ExternalOutput").ap()
    program(nc, ins, out)
    r = run_bass_kernel_spmd(nc, [feed], core_ids=[0])
    return r.results[0]["out"]
```
